# Optimizing a Trainium2 kernel written in Bass

```python
import numpy as np
import jax
import jax.numpy as jnp

def _softmax(x, axis=-1):
    return jax.nn.softmax(x, axis=axis)

def _gelu(x):
    return jax.nn.gelu(x, approximate=True)

def _silu(x):
    return jax.nn.silu(x)

def _sigmoid(x):
    return jax.nn.sigmoid(x)

def _layernorm(x, axis=-1, eps=1e-05):
    m = jnp.mean(x, axis=axis, keepdims=True)
    v = jnp.var(x, axis=axis, keepdims=True)
    return (x - m) / jnp.sqrt(v + eps)

def _scatter_add(tgt, idx, src, axis=0):
    return tgt.at[idx].add(src)

def _segment_sum(src, seg, n):
    return jax.ops.segment_sum(src, seg, n)
kernel_name = 'mk_decoder_postln_d1_seqx_r4_ff873d'

def setup_inputs(seed: int=0):
    np.random.seed(seed)
    _w = jnp.asarray

    def _rec_inputs():
        import jax
        import jax.numpy as jnp
        _rk = jax.random.key(seed)
        x = -0.0003929 + 0.9999 * jax.random.normal(jax.random.fold_in(_rk, 1), (8, 112, 256), jnp.float32)
        _lenS = 112 - jax.random.randint(jax.random.fold_in(_rk, 7), (8,), 0, max(1, 112 // 4) + 1, jnp.int32)
        _lenS2 = 375 - jax.random.randint(jax.random.fold_in(_rk, 8), (8,), 0, max(1, 375 // 4) + 1, jnp.int32)
        _ctx_1024P = jax.random.normal(jax.random.fold_in(_rk, 11), (8, 16, 256), jnp.float32)
        _ctx_1024c = jax.random.dirichlet(jax.random.fold_in(_rk, 511), 0.3 * jnp.ones((16,), jnp.float32), (8, 375))
        _ctx_1024t = jnp.einsum('bsk,bkd->bsd', _ctx_1024c, _ctx_1024P)
        _ctx_1024t = _ctx_1024t * jax.lax.rsqrt(jnp.mean(jnp.square(_ctx_1024t)) + 1e-12) * 0.953939
        ctx_1024 = 4.13588e-05 + 0.999923 * (_ctx_1024t + 0.3 * jax.random.normal(jax.random.fold_in(_rk, 611), (8, 375, 256), jnp.float32))
        return (x, ctx_1024)
    x, ctx_1024 = _rec_inputs()

    def _L0_attn_setup():
        import jax, jax.numpy as jnp
        import numpy as np
        HEADS = 16
        key = jax.random.key(seed)
        ks = jax.random.split(key, 6)
        b, n, c = (4, 512, 256)
        h = 256
        s = 0.02
        return {'x': jax.random.normal(ks[0], (b, n, c), jnp.float32), 'Wq': jax.random.normal(ks[1], (h, c), jnp.float32) * s, 'Wk': jax.random.normal(ks[2], (h, c), jnp.float32) * s, 'Wv': jax.random.normal(ks[3], (h, c), jnp.float32) * s, 'Wout': jax.random.normal(ks[4], (c, h), jnp.float32) * s, 'bout': jnp.zeros((c,), jnp.float32)}
    _L0_attn_all = _L0_attn_setup()
    _L0_attn_in = {k: v for k, v in _L0_attn_all.items() if k in ('Wq', 'Wk', 'Wv', 'Wout', 'bout')}
    del _L0_attn_all

    def _L0_xattn_setup():
        import jax, jax.numpy as jnp
        import numpy as np
        key = jax.random.key(seed)
        k1, k2 = jax.random.split(key)
        B, L, V, D = (8, 512, 256, 256)
        hidden_states = jax.random.normal(k1, (B, L, D), dtype=jnp.float32)
        visual_hidden_state = jax.random.normal(k2, (B, V, D), dtype=jnp.float32)
        return {'hidden_states': hidden_states, 'visual_hidden_state': visual_hidden_state}
    _L0_xattn_all = _L0_xattn_setup()
    _L0_xattn_in = {k: v for k, v in _L0_xattn_all.items() if k in ()}
    del _L0_xattn_all

    def _L0_ffn_setup():
        import jax, jax.numpy as jnp
        import numpy as np
        EMB = 256
        FF = 4 * EMB

        def _ternary(w):
            scale = jnp.maximum(jnp.mean(jnp.abs(w)), 1e-08)
            w_t = jnp.clip(jnp.round(w / scale), -1.0, 1.0)
            return w + jax.lax.stop_gradient(w_t - w)
        key = jax.random.key(seed)
        kx, k1, k2, kb1, kb2 = jax.random.split(key, 5)
        x = jax.random.normal(kx, (4, 512, EMB), dtype=jnp.float32)
        lim1 = 1.0 / np.sqrt(EMB)
        lim2 = 1.0 / np.sqrt(FF)
        W1 = jax.random.uniform(k1, (FF, EMB), jnp.float32, -lim1, lim1)
        b1 = jax.random.uniform(kb1, (FF,), jnp.float32, -lim1, lim1)
        W2 = jax.random.uniform(k2, (EMB, FF), jnp.float32, -lim2, lim2)
        b2 = jax.random.uniform(kb2, (EMB,), jnp.float32, -lim2, lim2)
        return {'x': x, 'W1': W1, 'b1': b1, 'W2': W2, 'b2': b2}
    _L0_ffn_all = _L0_ffn_setup()
    _L0_ffn_in = {k: v for k, v in _L0_ffn_all.items() if k in ('W1', 'b1', 'W2', 'b2')}
    del _L0_ffn_all
    return {'x': x, 'ctx_1024': ctx_1024, 'L0_attn_Wq': _L0_attn_in['Wq'], 'L0_attn_Wk': _L0_attn_in['Wk'], 'L0_attn_Wv': _L0_attn_in['Wv'], 'L0_attn_Wout': _L0_attn_in['Wout'], 'L0_attn_bout': _L0_attn_in['bout'], 'L0_ffn_W1': _L0_ffn_in['W1'], 'L0_ffn_b1': _L0_ffn_in['b1'], 'L0_ffn_W2': _L0_ffn_in['W2'], 'L0_ffn_b2': _L0_ffn_in['b2']}

def reference(x, ctx_1024, L0_attn_Wq, L0_attn_Wk, L0_attn_Wv, L0_attn_Wout, L0_attn_bout, L0_ffn_W1, L0_ffn_b1, L0_ffn_W2, L0_ffn_b2):
    import jax
    import jax.numpy as jnp

    def _L0_attn_ref(x, Wq, Wk, Wv, Wout, bout):
        import jax, jax.numpy as jnp
        import numpy as np
        HEADS = 16
        b, n, c = x.shape
        m = HEADS
        d = Wq.shape[0] // m
        q = jnp.einsum('bnc,hc->bnh', x, Wq).reshape(b, n, m, d)
        k = jnp.einsum('bnc,hc->bnh', x, Wk).reshape(b, n, m, d)
        v = jnp.einsum('bnc,hc->bnh', x, Wv).reshape(b, n, m, d)
        scale = d ** (-0.25)
        weight = jnp.einsum('bimd,bjmd->bmij', q * scale, k * scale)
        weight = jax.nn.softmax(weight, axis=-1)
        a = jnp.einsum('bmij,bjmd->bimd', weight, v).reshape(b, n, m * d)
        return jnp.einsum('bnh,ch->bnc', a, Wout) + bout

    def _L0_xattn_ref(hidden_states, visual_hidden_state):
        import jax, jax.numpy as jnp
        import numpy as np
        scores = jnp.einsum('bld,bvd->blv', hidden_states, visual_hidden_state)
        probs = jax.nn.softmax(scores, axis=-1)
        return jnp.einsum('blv,bvd->bld', probs, visual_hidden_state)

    def _L0_ffn_ref(x, W1, b1, W2, b2):
        import jax, jax.numpy as jnp
        import numpy as np
        EMB = 256
        FF = 4 * EMB

        def _ternary(w):
            scale = jnp.maximum(jnp.mean(jnp.abs(w)), 1e-08)
            w_t = jnp.clip(jnp.round(w / scale), -1.0, 1.0)
            return w + jax.lax.stop_gradient(w_t - w)
        h = jnp.einsum('bsd,fd->bsf', x, _ternary(W1)) + b1
        h = jax.nn.gelu(h, approximate=False)
        out = jnp.einsum('bsf,df->bsd', h, _ternary(W2)) + b2
        return out
    x = _layernorm(x + _L0_attn_ref(x, L0_attn_Wq, L0_attn_Wk, L0_attn_Wv, L0_attn_Wout, L0_attn_bout), axis=-1)
    x = _layernorm(x + _L0_xattn_ref(x, ctx_1024), axis=-1)
    x = _layernorm(x + _L0_ffn_ref(x, L0_ffn_W1, L0_ffn_b1, L0_ffn_W2, L0_ffn_b2), axis=-1)
    return x

_drawn_inputs = setup_inputs


def setup_inputs(seed=0):
    import zlib

    import numpy as np

    out = dict(_drawn_inputs(seed))
    spreads = {'L0_attn_bout': (0.0, 0.1)}
    factors = {'L0_attn_Wq': 8.0, 'L0_attn_Wk': 8.0, 'L0_ffn_b1': 24.699, 'L0_ffn_b2': 64.0}
    for name, (base, spread) in spreads.items():
        noise = np.random.default_rng([zlib.crc32(name.encode()), seed]).standard_normal(out[name].shape)
        drawn = base * np.exp(spread * noise) if base else spread * noise
        out[name] = jnp.asarray(drawn.astype(out[name].dtype))
    for name, factor in factors.items():
        out[name] = (out[name] * factor).astype(out[name].dtype)
    return out
```

```python
from contextlib import ExitStack

import concourse.bass as bass
from concourse import mybir

F32 = mybir.dt.float32
F32R = mybir.dt.float32r
BF16 = mybir.dt.bfloat16
F16 = mybir.dt.float16
ALU = mybir.AluOpType
ACT = mybir.ActivationFunctionType
AX = mybir.AxisListType

P = 128
EPS = 1e-5
HEADS = 16
BANK = 512
Q_PARTS = (0, 0, 1, 1, 0, 2)
K_PARTS = (0, 1, 0, 1, 2, 0)
GROUPS = len(Q_PARTS)
MAX_ROW = 96


def order(batches):
    lag = [("M", 1), ("S", 0), ("C", 4), ("D", 4), ("A", 3), ("G", 5), ("T", 1), ("V", 2),
           ("B", 3), ("E", 4), ("L1", 3), ("F", 4), ("L2", 4)]
    half = batches // 2
    steps = []
    for i in range(batches + 5):
        steps += [(s, i - l) for s, l in lag if 0 <= i - l < batches]
        if i == half + 4:
            steps.append(("H", 0))
        if half + 4 < i <= 2 * half + 4:
            if i > half + 5:
                steps.append(("L3", i - half - 6))
            steps.append(("I", i - half - 5))
    steps += [("H", 1), ("L3", half - 1)]
    for b in range(half, batches):
        steps.append(("I", b))
        if b > half:
            steps.append(("L3", b - 1))
    steps.append(("L3", batches - 1))
    return steps


def decoder_layer(nc, x, xT, ctx, ctxT, WqT, WkT, WvT, WoT, bo, W1T, b1, W2T, b2, out):
    NB, N, C = x.shape
    S = ctx.shape[1]
    FF = W1T.shape[1]
    D = C // HEADS
    CC = C // P
    FC = FF // P
    SP_ = 125
    SC = S // SP_
    HPC = P // D
    HB = NB // 2
    HN = HB * N
    CR = 4
    QUADS = HEADS // 4
    assert CC * P == C and SC * SP_ == S and HN <= BANK and 4 * N <= BANK and GROUPS * D == MAX_ROW
    ORDER = order(NB)

    with ExitStack() as ctx_:
        def sb(name, shape, dt=F32):
            return ctx_.enter_context(nc.sbuf_tensor(name, shape, dt))

        def sem(name):
            return ctx_.enter_context(nc.semaphore(name))

        x_sb = sb("x_sb", [N, NB, C])
        wo = sb("wo", [P, CC, C])
        w1 = sb("w1", [P, CC * FF]); w2 = sb("w2", [P, FC * C])
        t1 = sb("t1", [P, CC, FF], F16)
        t2 = sb("t2", [P, FC, C], F32R)
        wtmp = sb("wtmp", [P, 2, CC * FF])
        wsum = sb("wsum", [P, 2]); thr = sb("thr", [P, 6])
        bo_bc = sb("bo_bc", [N, C]); b2_bc = sb("b2_bc", [N, C])
        b1_sb = sb("b1_sb", [P, FC])
        ctx_sb = sb("ctx_sb", [SP_, SC, CR, C])
        ctxT_sb = sb("ctxT_sb", [P, CC, CR, S])
        ones = sb("ones", [P, P]); identf = sb("identf", [P, P])
        identb = sb("identb", [P, P], BF16)
        half_neg = sb("half_neg", [P, 1])
        v_sb = sb("v_sb", [N, NB, HEADS, D + 1])
        mx = sb("mx", [N, 2, HEADS]); mcat = sb("mcat", [N, 2, 2 * HEADS], BF16)
        sel = sb("sel", [2 * HEADS, HEADS, N], BF16)
        mT = sb("mT", [2 * HEADS, 2, N], BF16)
        pT = sb("pT", [N, 2, HEADS, N])
        rden = sb("rden", [N, 2, HEADS]); a_sb = sb("a_sb", [N, 2, C])
        aT = sb("aT", [P, 2, CC, N])
        stats = sb("stats", [N, 3, 6]); mv = sb("mv", [N, 3, 2]); rstd = sb("rstd", [N, 3, 2])
        nmax = sb("nmax", [N, 2]); den = sb("den", [N, 2]); rdx = sb("rdx", [N, 2])

        with ExitStack() as early:
            def sbe(name, shape, dt=F32):
                return early.enter_context(nc.sbuf_tensor(name, shape, dt))
            xT_sb = sbe("xT_sb", [P, CC, NB * N])
            wq = sbe("wq", [P, CC, C]); wk = sbe("wk", [P, CC, C]); wv = sbe("wv", [P, CC, C])
            qk = [sbe(f"qk_part{n}", [P, 2, CC, NB * N], BF16) for n in range(3)]
            rest = sbe("rest", [P, 2, HN])
        y = sb("y", [N, 3, C])
        x1 = sb("x1", [N, 3, C]); x1T = sb("x1T", [P, 2, CC, N])
        px = sb("px", [N, 2, S]); pxT = sb("pxT", [SP_, 2, SC, N])
        x2 = sb("x2", [N, NB, C])
        x2h = sb("x2h", [P, CC, NB * N], F16); x2l = sb("x2l", [P, CC, NB * N], F16)
        h = sb("h", [P, 2, HN])
        o_sb = sb("o_sb", [N, 2, C])
        early_bytes = 4 * (CC * NB * N + 3 * CC * C + 2 * HN) + 3 * 2 * 2 * CC * NB * N
        late_bytes = 4 * (3 * C + 3 * C + 2 * CC * N + 2 * S + 2 * SC * N + NB * C + 2 * HN + 2 * C) \
            + 2 * 2 * CC * NB * N
        sb("gap", [P, max(early_bytes - late_bytes, 4) // 4 + 16])

        with ExitStack() as attention:
            qs = attention.enter_context(nc.sbuf_tensor("qs", [P, HEADS, NB * N], BF16))
            ks = attention.enter_context(nc.sbuf_tensor("ks", [P, HEADS, NB * N], BF16))
        hh = sb("hh", [P, FC, HN], F32R); hl = sb("hl", [P, FC, HN], F32R)

        parts = nc.dram_tensor("parts", (2, 2, 3, HEADS * D, HN), BF16, kind="Internal").ap()

        banks = ctx_.enter_context(nc.psum_tensor("banks", [P, 8, BANK], F32))
        bank_s = [0, 1]
        bank_t = [2, 3]
        bank_v = 4
        bank_tp = 5
        bank_mm = [6, 7]

        in_qk = sem("in_qk"); in_xT = [sem("in_xT0"), sem("in_xT1")]; in_wv = sem("in_wv")
        in_ffn = sem("in_ffn"); in_x = sem("in_x"); in_wo = sem("in_wo")
        in_b1 = sem("in_b1")
        in_ctxT = [sem(f"in_ctxT{b}") for b in range(NB)]; in_ctx = [sem(f"in_ctx{b}") for b in range(NB)]
        const_ready = sem("const_ready"); const_step = sem("const_step")
        proj_done = sem("proj_done"); part1_done = sem("part1_done"); rest_done = sem("rest_done")
        part2_done = sem("part2_done"); part3_done = sem("part3_done")
        parted = [[sem(f"parted{i}{j}") for j in range(2)] for i in range(2)]
        sel_done = sem("sel_done"); sel_placed = sem("sel_placed")
        stacked = [sem("stacked0"), sem("stacked1")]
        v_done = sem("v_done"); v_kept = sem("v_kept")
        wsum_done = sem("wsum_done"); wtotal_done = sem("wtotal_done"); thr_done = sem("thr_done")
        tern_step = sem("tern_step"); tern_done = sem("tern_done")
        xb_done = sem("xb_done")
        s_done = sem("s_done"); max_done = sem("max_done"); mcat_step = sem("mcat_step")
        mcat_done = sem("mcat_done"); m_turned = sem("m_turned"); m_placed = [sem("m_placed0"), sem("m_placed1")]
        t_done = sem("t_done"); exp_done = sem("exp_done"); pv_done = sem("pv_done")
        rden_done = sem("rden_done"); a_done = sem("a_done")
        turned = sem("turned")
        tp_free = sem("tp_free")
        mm_done = sem("mm_done")
        x2h_done = sem("x2h_done"); thr_step = sem("thr_step")
        y_done = sem("y_done"); bn_done = sem("bn_done"); var_done = sem("var_done")
        eps_done = sem("eps_done"); rstd_done = sem("rstd_done"); ln_done = sem("ln_done")
        nmax_done = sem("nmax_done"); px_done = sem("px_done"); rdx_done = sem("rdx_done")
        x2b_done = sem("x2b_done")
        hid_done = sem("hid_done"); gelu_done = sem("gelu_done"); hh_done = sem("hh_done"); hl_done = sem("hl_done")
        stored = [sem("stored0"), sem("stored1")]

        block = ctx_.enter_context(nc.Block())

        TURNS = [st for st in ORDER if st[0] in "MACEG"]
        RESULTS = [st for st in ORDER if st[0] in "BDFI"]
        SUMS = [st for st in ORDER if st[0] in "BFI"]
        ENDS = [st for st in ORDER if st[0] in ("L1", "L2", "L3")]

        SUM_OF = {"L1": "B", "L2": "F", "L3": "I"}
        END_OF = {s: l for l, s in SUM_OF.items()}

        def count(uses, stage, b):
            return uses.index((stage, b)) + 1

        def bank_of(stage, b):
            return (count(RESULTS, stage, b) - 1) % 2

        def cols(b):
            return slice(b * N, (b + 1) * N)

        @block.sync
        def _(sp):
            sp.dma_start(wq[:, :, :], WqT.rearrange("(c p) n -> p c n", p=P)).then_inc(in_qk, 16)
            xv = xT.rearrange("(c p) n -> p c n", p=P)
            sp.dma_start(xT_sb[:, :, 0:HN], xv[:, :, 0:HN]).then_inc(in_xT[0], 16)
            sp.dma_start(wk[:, :, :], WkT.rearrange("(c p) n -> p c n", p=P)).then_inc(in_qk, 16)
            sp.dma_start(xT_sb[:, :, HN:2 * HN], xv[:, :, HN:2 * HN]).then_inc(in_xT[1], 16)
            sp.dma_start(wv[:, :, :], WvT.rearrange("(c p) n -> p c n", p=P)).then_inc(in_wv, 16)
            sp.dma_start(w1[:, :].rearrange("p (c f) -> p c f", c=CC),
                         W1T.rearrange("(c p) f -> p c f", p=P)).then_inc(in_ffn, 16)
            sp.dma_start(w2[:, :].rearrange("p (c n) -> p c n", c=FC),
                         W2T.rearrange("(c p) n -> p c n", p=P)).then_inc(in_ffn, 16)

            def stack(half):
                cs = slice(half * HN, (half + 1) * HN)
                for side in range(2):
                    for r, made in enumerate((part1_done, part2_done, part3_done)):
                        sp.wait_ge(made, CC * (2 * half + side + 1))
                        sp.dma_start(parts[half, side, r].rearrange("(c p) n -> p c n", p=P),
                                     qk[r][:, side, :, cs]).then_inc(parted[half][side], 16)
                for side, (dst, rows) in enumerate(((qs, Q_PARTS), (ks, K_PARTS))):
                    sp.wait_ge(parted[half][side], 16 * 3)
                    for g in range(GROUPS):
                        sp.dma_start(dst[g * D:(g + 1) * D, :, cs],
                                     parts[half, side, rows[g]].rearrange("(h d) n -> d h n", d=D)
                                     ).then_inc(stacked[half], 16)

            stack(0)
            sp.wait_ge(sel_done, 3)
            for b in range(NB):
                sp.dma_start(ks[MAX_ROW:P, :, cols(b)], sel[:, :, :]).then_inc(sel_placed, 16)
            sp.dma_start(x_sb[:, :, :], x.rearrange("b n c -> n b c")).then_inc(in_x, 16)
            sp.dma_start(bo_bc[:, :], bo.partition_broadcast(N)).then_inc(in_x, 16)
            sp.dma_start(b2_bc[:, :], b2.partition_broadcast(N)).then_inc(in_x, 16)
            sp.dma_start(b1_sb[:, :], b1).then_inc(in_b1, 16)
            stack(1)
            sp.dma_start(wo[:, :, :], WoT.rearrange("(c p) n -> p c n", p=P)).then_inc(in_wo, 16)

            def load_context(b):
                if b >= CR:
                    sp.wait_ge(mm_done, count(RESULTS, "F", b - CR))
                sp.dma_start(ctxT_sb[:, :, b % CR, :],
                             ctxT[b].rearrange("(c p) s -> p c s", p=P)).then_inc(in_ctxT[b], 16)
                sp.dma_start(ctx_sb[:, :, b % CR, :],
                             ctx[b].rearrange("(c p) n -> p c n", p=SP_)).then_inc(in_ctx[b], 16)

            for stage, b in ORDER:
                if stage == "M":
                    sp.wait_ge(tp_free, count(TURNS, "M", b))
                    sp.dma_start(qs[MAX_ROW:P, :, cols(b)],
                                 mT[:, b % 2, :].unsqueeze(1).broadcast_to((2 * HEADS, HEADS, N))).then_inc(m_placed[b % 2], 16)
                if stage == "S":
                    load_context(b)
                if stage == "L3":
                    sp.wait_ge(ln_done, count(ENDS, "L3", b))
                    sp.dma_start(out[b], o_sb[:, b % 2, :]).then_inc(stored[b % 2], 16)
            for k in range(2):
                sp.wait_ge(stored[k], 16 * HB)

        @block.gpsimd
        def _(pool):
            pool.memset(half_neg[:, :], -0.5).then_inc(const_ready, 1)
            pool.memset(ones[:, :], 1.0).then_inc(const_ready, 1)
            pool.memset(identf[:, :], 0.0).then_inc(const_step, 1)
            pool.memset(identb[:, :], 0.0).then_inc(const_step, 1)
            pool.wait_ge(const_step, 2)
            for ident in (identf, identb):
                pool.affine_select(out=ident[:, :], in_=ident[:, :], compare_op=ALU.not_equal, fill=1.0,
                                   base=0, pattern=[[-1, P]], channel_multiplier=1).then_inc(const_ready, 1)
            pool.memset(sel[:, :, :], 0.0).then_inc(sel_done, 1)
            for r in range(2):
                pool.wait_ge(sel_done, r + 1)
                pool.affine_select(out=sel[:, :, :], in_=sel[:, :, :], compare_op=ALU.not_equal, fill=-1.0,
                                   base=-r * HEADS, pattern=[[-1, HEADS], [0, N]],
                                   channel_multiplier=1).then_inc(sel_done, 1)
            pool.wait_ge(sel_done, 3)
            pool.memset(v_sb[:, :, :, D:D + 1], 1.0).then_inc(const_ready, 1)

            pool.wait_ge(in_x, 48)
            pool.tensor_tensor(x_sb[:, :, :], x_sb[:, :, :],
                               bo_bc[:, :].unsqueeze(1).broadcast_to((N, NB, C)), ALU.add).then_inc(xb_done, 1)

            below, above = wtmp[:, 0, :], wtmp[:, 1, :]
            pool.wait_ge(thr_done, 2)
            for n, (w, t) in enumerate(((w1, t1), (w2, t2))):
                if n:
                    pool.wait_ge(tern_done, 1)
                pool.tensor_scalar(below, w[:, :], thr[:, 2 + n:3 + n], None, ALU.is_lt).then_inc(tern_step, 1)
                pool.tensor_scalar(above, w[:, :], thr[:, n:n + 1], None, ALU.is_gt).then_inc(tern_step, 1)
                pool.wait_ge(tern_step, 2 * (n + 1))
                pool.tensor_tensor(t[:, :, :].rearrange("p c n -> p (c n)"), above, below,
                                   ALU.subtract).then_inc(tern_done, 1)

            sums = 0
            for stage, b in ORDER:
                if stage in ("B", "F", "I"):
                    k = sums % 3
                    sums += 1
                    pool.wait_ge(var_done, sums)
                    pool.tensor_scalar(rstd[:, k, 0:1], mv[:, k, 1:2], EPS, None, ALU.add).then_inc(eps_done, 1)
                    pool.wait_ge(eps_done, sums)
                    pool.tensor_tensor(rstd[:, k, 1:2], rstd[:, k, 0:1], half_neg[0:N, :],
                                       ALU.pow).then_inc(rstd_done, 1)
                if stage == "G":
                    pool.wait_ge(turned, count(TURNS, "G", b))
                    pool.tensor_tensor(x2[:, b, :], x2[:, b, :], b2_bc[:, :], ALU.add).then_inc(x2b_done, 1)

        @block.scalar
        def _(act):
            pieces = [(half, side, c) for half in range(2) for side in range(2) for c in range(CC)]

            def part2(n):
                half, side, c = pieces[n]
                act.wait_ge(rest_done, n + 1)
                act.activation(qk[1][:, side, c, half * HN:(half + 1) * HN], rest[:, n % 2, :],
                               ACT.Copy).then_inc(part2_done, 1)

            for n, (half, side, c) in enumerate(pieces):
                act.wait_ge(proj_done, n + 1)
                act.activation(qk[0][:, side, c, half * HN:(half + 1) * HN], banks[:, n % 4, 0:HN],
                               ACT.Copy).then_inc(part1_done, 1)
                if n:
                    part2(n - 1)
                if n == len(pieces) // 2:
                    act.wait_ge(in_ffn, 32)
                    for k, w in enumerate((w1, w2)):
                        act.activation(wtmp[:, k, :], w[:, :], ACT.Abs,
                                       accum_out=wsum[:, k:k + 1]).then_inc(wsum_done, 1)
            part2(len(pieces) - 1)

            act.wait_ge(const_ready, 5)
            for b in range(NB):
                act.wait_ge(v_done, b + 1)
                act.activation(v_sb[:, b, :, 0:D],
                               banks[0:N, 4 + b % 4, 0:C].rearrange("n (h d) -> n h d", d=D),
                               ACT.Copy).then_inc(v_kept, 1)

            hidden = 0
            for stage, b in ORDER:
                if stage == "T":
                    for q in range(QUADS):
                        n = QUADS * b + q
                        act.wait_ge(t_done, n + 1)
                        if b >= 2:
                            act.wait_ge(pv_done, b - 1)
                        act.activation(pT[:, b % 2, 4 * q:4 * q + 4, :],
                                       banks[0:N, bank_t[n % 2], 0:4 * N].rearrange("k (h n) -> k h n", n=N),
                                       ACT.Exp, scale=float(D) ** -0.5).then_inc(exp_done, 1)
                if stage == "C" and b == 0:
                    act.wait_ge(stacked[1], 16 * GROUPS * 2)
                if stage in ("A", "C"):
                    use = count(TURNS, stage, b)
                    act.wait_ge(turned, use)
                    if b >= 2:
                        act.wait_ge(mm_done, count(RESULTS, "B" if stage == "A" else "D", b - 2))
                    act.activation((aT if stage == "A" else x1T)[:, b % 2, :, :],
                                   banks[:, bank_tp, 0:CC * N].rearrange("p (c n) -> p c n", n=N),
                                   ACT.Copy).then_inc(tp_free, 1)
                if stage == "D":
                    act.wait_ge(nmax_done, b + 1)
                    if b >= 2:
                        act.wait_ge(turned, count(TURNS, "E", b - 2))
                        act.wait_ge(rdx_done, b - 1)
                    act.activation(px[:, b % 2, :], banks[0:N, bank_mm[bank_of("D", b)], 0:S], ACT.Exp,
                                   bias=nmax[:, b % 2:b % 2 + 1],
                                   accum_out=den[:, b % 2:b % 2 + 1]).then_inc(px_done, 1)
                if stage == "G":
                    act.wait_ge(turned, count(TURNS, "G", b))
                    act.activation(x2h[:, :, cols(b)],
                                   banks[:, bank_tp, 0:CC * N].rearrange("p (c n) -> p c n", n=N),
                                   ACT.Copy).then_inc(x2h_done, 1)
                if stage == "H":
                    act.wait_ge(in_b1, 16)
                    for f in range(FC):
                        act.wait_ge(hid_done, hidden + 1)
                        if hidden >= 2:
                            act.wait_ge(hl_done, hidden - 1)
                        act.activation(h[:, hidden % 2, :], banks[:, bank_s[hidden % 2], 0:HN], ACT.Gelu,
                                       bias=b1_sb[:, f:f + 1]).then_inc(gelu_done, 1)
                        hidden += 1

        @block.vector
        def _(dve):
            pieces = [(half, side, c) for half in range(2) for side in range(2) for c in range(CC)]

            def part3(n):
                half, side, c = pieces[n]
                cs = slice(half * HN, (half + 1) * HN)
                dve.wait_ge(part2_done, n + 1)
                dve.tensor_tensor(qk[2][:, side, c, cs], rest[:, n % 2, :], qk[1][:, side, c, cs],
                                  ALU.subtract).then_inc(part3_done, 1)

            for n, (half, side, c) in enumerate(pieces):
                dve.wait_ge(part1_done, n + 1)
                if n >= 2:
                    dve.wait_ge(part3_done, n - 1)
                dve.tensor_tensor(rest[:, n % 2, :], banks[:, n % 4, 0:HN],
                                  qk[0][:, side, c, half * HN:(half + 1) * HN],
                                  ALU.subtract).then_inc(rest_done, 1)
                if n:
                    part3(n - 1)
            part3(len(pieces) - 1)

            dve.wait_ge(wtotal_done, 1)
            dve.tensor_scalar(thr[:, 4:6], banks[:, 5, 0:2], 1.0 / (C * FF), 1e-8,
                              ALU.mult, ALU.max).then_inc(thr_step, 1)
            dve.wait_ge(thr_step, 1)
            dve.tensor_scalar(thr[:, 0:2], thr[:, 4:6], 0.5, None, ALU.mult).then_inc(thr_done, 1)
            dve.tensor_scalar(thr[:, 2:4], thr[:, 4:6], -0.5, None, ALU.mult).then_inc(thr_done, 1)

            sums = hidden = 0

            def statistics(k):
                dve.wait_ge(y_done, sums)
                dve.bn_stats(stats[:, k, :], y[:, k, :]).then_inc(bn_done, 1)
                dve.wait_ge(bn_done, sums)
                dve.bn_aggr(mv[:, k, :], stats[:, k, :]).then_inc(var_done, 1)

            for stage, b in ORDER:
                if stage == "S":
                    if b >= 2:
                        dve.wait_ge(mcat_done, b - 1)
                    for q in range(QUADS):
                        n = QUADS * b + q
                        dve.wait_ge(s_done, n + 1)
                        dve.tensor_reduce(mx[:, b % 2, 4 * q:4 * q + 4],
                                          banks[0:N, bank_s[n % 2], 0:4 * N].rearrange("q (h k) -> q h k", k=N),
                                          AX.X, ALU.max).then_inc(max_done, 1)
                    dve.wait_ge(max_done, QUADS * (b + 1))
                    dve.tensor_copy(mcat[:, b % 2, 0:HEADS], mx[:, b % 2, :]).then_inc(mcat_step, 1)
                    dve.wait_ge(mcat_step, b + 1)
                    dve.tensor_tensor(mcat[:, b % 2, HEADS:2 * HEADS], mx[:, b % 2, :],
                                      mcat[:, b % 2, 0:HEADS], ALU.subtract).then_inc(mcat_done, 1)
                if stage == "M":
                    dve.wait_ge(turned, count(TURNS, "M", b))
                    if b >= 2:
                        dve.wait_ge(m_placed[b % 2], 16 * (b // 2))
                    dve.tensor_copy(mT[:, b % 2, :],
                                    banks[0:2 * HEADS, bank_tp, 0:N // 2].bitcast(BF16)).then_inc(tp_free, 1)
                if stage == "V":
                    av = banks[0:N, bank_v, 0:HEADS * (D + 1)].rearrange("n (h e) -> n h e", e=D + 1)
                    dve.wait_ge(pv_done, b + 1)
                    if b >= 2:
                        dve.wait_ge(a_done, b - 1)
                    dve.reciprocal(rden[:, b % 2, :], av[:, :, D]).then_inc(rden_done, 1)
                    if b >= 2:
                        dve.wait_ge(turned, count(TURNS, "A", b - 2))
                    dve.wait_ge(rden_done, b + 1)
                    dve.tensor_tensor(a_sb[:, b % 2, :].rearrange("n (h d) -> n h d", d=D), av[:, :, 0:D],
                                      rden[:, b % 2, :].unsqueeze(2).broadcast_to((N, HEADS, D)),
                                      ALU.mult).then_inc(a_done, 1)
                if stage == "D":
                    dve.wait_ge(mm_done, count(RESULTS, "D", b))
                    if b >= 2:
                        dve.wait_ge(px_done, b - 1)
                    dve.tensor_reduce(nmax[:, b % 2:b % 2 + 1], banks[0:N, bank_mm[bank_of("D", b)], 0:S],
                                      AX.X, ALU.max, negate=True).then_inc(nmax_done, 1)
                if stage == "E":
                    dve.wait_ge(turned, count(TURNS, "E", b))
                    if b >= 2:
                        dve.wait_ge(mm_done, count(RESULTS, "F", b - 2))
                    dve.tensor_copy(pxT[:, b % 2, :, :],
                                    banks[0:SP_, bank_tp, 0:SC * N].rearrange("p (c n) -> p c n", n=N)
                                    ).then_inc(tp_free, 1)
                    dve.wait_ge(px_done, b + 1)
                    dve.reciprocal(rdx[:, b % 2:b % 2 + 1], den[:, b % 2:b % 2 + 1]).then_inc(rdx_done, 1)
                if stage in ("B", "F", "I"):
                    k = sums % 3
                    sums += 1
                    bank = bank_of(stage, b)
                    if sums == 1:
                        dve.wait_ge(stacked[1], 16 * GROUPS * 2)
                    dve.wait_ge(mm_done, count(RESULTS, stage, b))
                    psum = banks[0:N, bank_mm[bank], 0:C]
                    if sums > 3:
                        dve.wait_ge(ln_done, count(ENDS, END_OF[SUMS[sums - 4][0]], SUMS[sums - 4][1]))
                    if stage == "B":
                        if b == 0:
                            dve.wait_ge(xb_done, 1)
                        dve.tensor_tensor(y[:, k, :], psum, x_sb[:, b, :], ALU.add).then_inc(y_done, 1)
                    if stage == "F":
                        dve.wait_ge(rdx_done, b + 1)
                        dve.scalar_tensor_tensor(y[:, k, :], psum, rdx[:, b % 2:b % 2 + 1], x1[:, b % 3, :],
                                                 ALU.mult, ALU.add).then_inc(y_done, 1)
                    if stage == "I":
                        dve.wait_ge(x2b_done, b + 1)
                        dve.tensor_tensor(y[:, k, :], psum, x2[:, b, :], ALU.add).then_inc(y_done, 1)
                    statistics(k)
                if stage in ("L1", "L2", "L3"):
                    use = count(SUMS, SUM_OF[stage], b)
                    k = (use - 1) % 3
                    dve.wait_ge(rstd_done, use)
                    if stage == "L1":
                        if b >= 3:
                            dve.wait_ge(turned, count(TURNS, "C", b - 3))
                        to = x1[:, b % 3, :]
                    if stage == "L2":
                        to = x2[:, b, :]
                    if stage == "L3":
                        if b >= 2:
                            dve.wait_ge(stored[b % 2], 16 * (b // 2))
                        to = o_sb[:, b % 2, :]
                    dve.tensor_scalar(to, y[:, k, :], mv[:, k, 0:1], rstd[:, k, 1:2], ALU.subtract,
                                      ALU.mult).then_inc(ln_done, 1)
                if stage == "G":
                    dve.wait_ge(x2h_done, b + 1)
                    dve.tensor_tensor(x2l[:, :, cols(b)],
                                      banks[:, bank_tp, 0:CC * N].rearrange("p (c n) -> p c n", n=N),
                                      x2h[:, :, cols(b)], ALU.subtract).then_inc(tp_free, 1)
                if stage == "H":
                    for f in range(FC):
                        if b and f == 0:
                            dve.wait_ge(mm_done, count(RESULTS, "I", HB - 1))
                        dve.wait_ge(gelu_done, hidden + 1)
                        dve.tensor_copy(hh[:, f, :], h[:, hidden % 2, :]).then_inc(hh_done, 1)
                        hidden += 1
                        dve.wait_ge(hh_done, hidden)
                        dve.tensor_tensor(hl[:, f, :], h[:, (hidden - 1) % 2, :], hh[:, f, :].bitcast(F32),
                                          ALU.subtract).then_inc(hl_done, 1)

        @block.tensor
        def _(pe):
            pe.wait_ge(in_qk, 32)
            n = 0
            for half in range(2):
                pe.wait_ge(in_xT[half], 16)
                for w in (wq, wk):
                    for m in range(CC):
                        if n >= 4:
                            pe.wait_ge(rest_done, n - 3)
                        for c in range(CC):
                            mm = pe.matmul(banks[:, n % 4, 0:HN], w[:, c, m * P:(m + 1) * P],
                                           xT_sb[:, c, half * HN:(half + 1) * HN],
                                           start=(c == 0), stop=(c == CC - 1))
                        mm.then_inc(proj_done, 1)
                        n += 1

            pe.wait_ge(const_ready, 2)
            pe.wait_ge(wsum_done, 2)
            pe.matmul(banks[:, 5, 0:2], ones[:, :], wsum[:, 0:2], start=True, stop=True).then_inc(wtotal_done, 1)
            pe.wait_ge(thr_step, 1)

            pe.wait_ge(in_wv, 16)
            for b in range(NB):
                if b >= 4:
                    pe.wait_ge(v_kept, b - 3)
                for c in range(CC):
                    mm = pe.matmul(banks[0:N, 4 + b % 4, 0:C], xT_sb[:, c, cols(b)], wv[:, c, :],
                                   start=(c == 0), stop=(c == CC - 1))
                mm.then_inc(v_done, 1)

            def bank_tp_ready(stage, b):
                use = count(TURNS, stage, b)
                if use > 1:
                    pe.wait_ge(tp_free, use - 1)

            def bank_mm_ready(stage, b):
                use = count(RESULTS, stage, b)
                if use > 2:
                    last, lb = RESULTS[use - 3]
                    if last == "D":
                        pe.wait_ge(px_done, lb + 1)
                    else:
                        pe.wait_ge(y_done, count(SUMS, last, lb))
                return banks[0:N, bank_mm[(use - 1) % 2], :]

            def turn(src, rows, parts):
                for c in range(parts):
                    w = src.shape[1] // parts
                    mm = pe.transpose(banks[0:w, bank_tp, c * rows:(c + 1) * rows],
                                      src[:, c * w:(c + 1) * w], identf[0:rows, 0:rows])
                mm.then_inc(turned, 1)

            pe.wait_ge(v_kept, NB)
            pe.wait_ge(rest_done, 8)
            pe.wait_ge(const_ready, 5)
            hidden = 0
            for stage, b in ORDER:
                if stage == "S":
                    if b % HB == 0:
                        pe.wait_ge(stacked[b // HB], 16 * GROUPS * 2)
                    for q in range(QUADS):
                        n = QUADS * b + q
                        if n >= 2:
                            pe.wait_ge(max_done, n - 1)
                        for j in range(4):
                            mm = pe.matmul(banks[0:N, bank_s[n % 2], j * N:(j + 1) * N],
                                           qs[0:MAX_ROW, 4 * q + j, cols(b)], ks[0:MAX_ROW, 4 * q + j, cols(b)],
                                           start=True, stop=True)
                        mm.then_inc(s_done, 1)
                if stage == "M":
                    pe.wait_ge(mcat_done, b + 1)
                    bank_tp_ready("M", b)
                    pe.transpose(banks[0:2 * HEADS, bank_tp, 0:N // 2].bitcast(BF16), mcat[:, b % 2, :],
                                 identb[0:N, 0:N]).then_inc(turned, 1)
                if stage == "T":
                    if b == 0:
                        pe.wait_ge(sel_placed, 16 * NB)
                    pe.wait_ge(m_placed[b % 2], 16 * (b // 2 + 1))
                    for q in range(QUADS):
                        n = QUADS * b + q
                        if n >= 2:
                            pe.wait_ge(exp_done, n - 1)
                        for j in range(4):
                            mm = pe.matmul(banks[0:N, bank_t[n % 2], j * N:(j + 1) * N],
                                           ks[:, 4 * q + j, cols(b)],
                                           qs[:, 4 * q + j, cols(b)], start=True, stop=True)
                        mm.then_inc(t_done, 1)
                if stage == "V":
                    pe.wait_ge(exp_done, QUADS * (b + 1))
                    if b:
                        pe.wait_ge(a_done, b)
                    for hd in range(HEADS):
                        mm = pe.matmul(banks[0:N, bank_v, hd * (D + 1):(hd + 1) * (D + 1)],
                                       pT[:, b % 2, hd, :], v_sb[:, b, hd, :], start=True, stop=True)
                    mm.then_inc(pv_done, 1)
                if stage == "A":
                    pe.wait_ge(a_done, b + 1)
                    bank_tp_ready("A", b)
                    turn(a_sb[:, b % 2, :], N, CC)
                if stage == "B":
                    pe.wait_ge(tp_free, count(TURNS, "A", b))
                    if b == 0:
                        pe.wait_ge(in_wo, 16)
                    to = bank_mm_ready("B", b)
                    for c in range(CC):
                        mm = pe.matmul(to[:, 0:C], aT[:, b % 2, c, :], wo[:, c, :],
                                       start=(c == 0), stop=(c == CC - 1))
                    mm.then_inc(mm_done, 1)
                if stage == "C":
                    pe.wait_ge(ln_done, count(ENDS, "L1", b))
                    bank_tp_ready("C", b)
                    turn(x1[:, b % 3, :], N, CC)
                if stage == "D":
                    pe.wait_ge(tp_free, count(TURNS, "C", b))
                    pe.wait_ge(in_ctxT[b], 16)
                    to = bank_mm_ready("D", b)
                    for c in range(CC):
                        mm = pe.matmul(to[:, 0:S], x1T[:, b % 2, c, :], ctxT_sb[:, c, b % CR, :],
                                       start=(c == 0), stop=(c == CC - 1))
                    mm.then_inc(mm_done, 1)
                if stage == "E":
                    pe.wait_ge(px_done, b + 1)
                    bank_tp_ready("E", b)
                    turn(px[:, b % 2, :], N, SC)
                if stage == "F":
                    pe.wait_ge(tp_free, count(TURNS, "E", b))
                    pe.wait_ge(in_ctx[b], 16)
                    to = bank_mm_ready("F", b)
                    for c in range(SC):
                        mm = pe.matmul(to[:, 0:C], pxT[:, b % 2, c, :], ctx_sb[:, c, b % CR, :],
                                       start=(c == 0), stop=(c == SC - 1))
                    mm.then_inc(mm_done, 1)
                if stage == "G":
                    pe.wait_ge(ln_done, count(ENDS, "L2", b))
                    bank_tp_ready("G", b)
                    turn(x2[:, b, :], N, CC)
                if stage == "H":
                    if b == 0:
                        pe.wait_ge(max_done, QUADS * NB)
                        pe.wait_ge(tern_done, 2)
                    pe.wait_ge(tp_free, count(TURNS, "G", HB * (b + 1) - 1))
                    for f in range(FC):
                        if hidden >= 2:
                            pe.wait_ge(gelu_done, hidden - 1)
                        mms = [(c, part) for c in range(CC) for part in (x2h, x2l)]
                        for i, (c, part) in enumerate(mms):
                            mm = pe.matmul(banks[:, bank_s[hidden % 2], 0:HN], t1[:, c, f * P:(f + 1) * P],
                                           part[:, c, b * HN:(b + 1) * HN],
                                           start=(i == 0), stop=(i == len(mms) - 1))
                        mm.then_inc(hid_done, 1)
                        hidden += 1
                if stage == "I":
                    pe.wait_ge(hl_done, FC * (b // HB + 1))
                    to = bank_mm_ready("I", b)
                    mms = [(f, part) for f in range(FC) for part in (hh, hl)]
                    for i, (f, part) in enumerate(mms):
                        mm = pe.matmul(to[:, 0:C], part[:, f, cols(b % HB)], t2[:, f, :],
                                       start=(i == 0), stop=(i == len(mms) - 1))
                    mm.then_inc(mm_done, 1)

    return nc


def kernel(**inputs):
    import numpy as np
    import concourse.bacc as bacc
    from concourse.bass_utils import run_bass_kernel_spmd

    a = {k: np.asarray(v) for k, v in inputs.items()}

    def turned(m):
        return np.ascontiguousarray(np.moveaxis(m, -1, -2))

    x, ctx = a["x"], a["ctx_1024"]
    arrays = {
        "x": x,
        "xT": turned(x.reshape(-1, x.shape[-1])),
        "ctx": ctx,
        "ctxT": turned(ctx),
        "WqT": turned(a["L0_attn_Wq"]), "WkT": turned(a["L0_attn_Wk"]), "WvT": turned(a["L0_attn_Wv"]),
        "WoT": turned(a["L0_attn_Wout"]), "bo": a["L0_attn_bout"],
        "W1T": turned(a["L0_ffn_W1"]), "b1": turned(a["L0_ffn_b1"].reshape(-1, P)),
        "W2T": turned(a["L0_ffn_W2"]), "b2": a["L0_ffn_b2"],
    }
    arrays = {f"in_{k}": np.ascontiguousarray(v) for k, v in arrays.items()}
    nc = bacc.Bacc("TRN2", target_bir_lowering=False, num_devices=1)
    args = [nc.dram_tensor(k, v.shape, mybir.dt.from_np(v.dtype), kind="ExternalInput").ap()
            for k, v in arrays.items()]
    args.append(nc.dram_tensor("out", x.shape, F32, kind="ExternalOutput").ap())
    decoder_layer(nc, *args)
    r = run_bass_kernel_spmd(nc, [arrays], core_ids=[0])
    return r.results[0]["out"]
```

```python
from contextlib import ExitStack

import concourse.bass as bass
from concourse import mybir

F32 = mybir.dt.float32
F32R = mybir.dt.float32r
BF16 = mybir.dt.bfloat16
F16 = mybir.dt.float16
ALU = mybir.AluOpType
ACT = mybir.ActivationFunctionType
AX = mybir.AxisListType

P = 128
EPS = 1e-5
HEADS = 16
BANK = 512
Q_PARTS = (0, 1, 2, 0, 1, 0)
K_PARTS = (0, 0, 0, 1, 1, 2)
GROUPS = len(Q_PARTS)
Q_RUNS = ((0, 0, 3), (3, 0, 2), (5, 0, 1))
K_RUNS = ((0, 0, 1), (1, 0, 1), (2, 0, 2), (4, 1, 2))
WARM_UP = 8
PIECES = 8
STACKS = (2, 2, 4)
FFN = (3, 2, 2, 1)


STEPS = """
K:0 R:0 K:1 U:0 R:1 U:1 Load:0 K:2 U:2
Sa:0 U:3 Sb:0
Sa:1 M:0 Sb:1 R:2 Ta:0 J:0 Tb:0 Load:1 M:1 U:4 U:5 V:0 U:6 Ta:1
Sa:2 W:0 U:7 Sb:2 Tb:1 A:0
Sa:3 M:2 J:1 B:0 V:1 L1:0 Ta:2 W:1 C:0 A:1 Sb:3 Tb:2 D:0 B:1 M:3 E:0 V:2 J:2 L1:1 F:0
Sa:4 J:3 Z:0 L2:0 Ta:3 C:1 W:2 Sb:4 G:0 A:2 Z:1 D:1 B:2 Tb:3
Sa:5 E:1 X:0 L1:2 V:3 M:4 Y:0 F:1 J:4 C:2 Y:1 W:3 Ta:4 Tb:4 Sb:5 A:3 L2:1 D:2 Y:2 G:1 B:3 E:2 Y:3 L1:3
    F:2 M:5 V:4
Sa:6 W:4 J:5 Ta:5 J:6 Sb:6 L2:2 C:3 A:4 Y:4 Tb:5 D:3 B:4
Sa:7 L1:4 E:3 M:6 V:5 Y:5 G:2 F:3 C:4 W:5 Ta:6 Y:6 Sb:7 J:7 Tb:6 A:5 D:4 L2:3 Y:7 H:0 B:5 H:1 G:3 V:6
    H:2 H:3 L1:5 E:4 H:4 H:5 F:4 M:7 H:6 L2:4 H:7 W:6 Ta:7 C:5 Tb:7 A:6 D:5 B:6 G:4 I:0 L1:6 L3:0 I:1
    I:2 H:8 E:5 H:9 H:10 F:5 H:11 H:12 L3:1 V:7 H:13 C:6 W:7 L2:5 D:6 L3:2 A:7 G:5 B:7 H:14 E:6 H:15
    L1:7 F:6 L2:6 C:7 I:3 D:7 I:4 L3:3 E:7 G:6 F:7 H:16 H:17 L2:7 H:18 H:19 H:20 H:21 H:22 H:23 L3:4 G:7
    I:5 L3:5 I:6 H:24 H:25 H:26 H:27 H:28 L3:6 H:29 H:30 H:31 I:7 L3:7
"""


def order(batches, chunks):
    steps = [(s.split(":")[0], int(s.split(":")[1])) for s in STEPS.split()]
    assert [b for s, b in steps if s == "B"] == list(range(batches))
    assert [b for s, b in steps if s == "H"] == list(range(chunks * len(FFN)))
    return steps


def decoder_layer(nc, x, xT, ctx, ctxT, WqT, WkT, WvT, WoT, bo, W1T, b1, W2T, b2, out):
    NB, N, C = x.shape
    S = ctx.shape[1]
    FF = W1T.shape[1]
    D = C // HEADS
    CC = C // P
    FC = FF // P
    SP_ = 125
    SC = S // SP_
    HPC = P // D
    FT = max(FFN) * N
    KT = max(STACKS) * N
    FIRST = [sum(FFN[:g]) for g in range(len(FFN) + 1)]
    START = [sum(STACKS[:p]) for p in range(len(STACKS) + 1)]
    GROUP_OF = [g for g, size in enumerate(FFN) for _ in range(size)]
    CR = 4
    HR = 4
    QUADS = HEADS // 4
    assert CC * P == C and SC * SP_ == S and max(FT, KT) <= BANK and FIRST[-1] == START[-1] == NB and 4 * N <= BANK and GROUPS * D <= P
    ORDER = order(NB, FC)

    with ExitStack() as ctx_:
        def sb(name, shape, dt=F32):
            return ctx_.enter_context(nc.sbuf_tensor(name, shape, dt))

        def sem(name):
            return ctx_.enter_context(nc.semaphore(name))

        x_sb = sb("x_sb", [N, NB, C])
        wo = sb("wo", [P, CC, C])
        t1 = sb("t1", [P, CC, FF], F16)
        t2 = sb("t2", [P, FC, C], F32R)
        wsum = sb("wsum", [P, 2]); thr = sb("thr", [P, 6])
        bo_bc = sb("bo_bc", [N, C]); b2_bc = sb("b2_bc", [N, C])
        b1_sb = sb("b1_sb", [P, FC])
        ctx_sb = sb("ctx_sb", [SP_, SC, CR, C])
        ctxT_sb = sb("ctxT_sb", [P, CC, CR, S])
        ones = sb("ones", [P, P]); identf = sb("identf", [P, P])
        identb = sb("identb", [P, P], BF16)
        half_neg = sb("half_neg", [P, 1])
        v_sb = sb("v_sb", [N, NB, HEADS, 32])
        mx = sb("mx", [N, 2, HEADS]); mcat = sb("mcat", [N, 2, 2 * HEADS], BF16)
        sel = sb("sel", [2 * HEADS, HEADS, N], BF16)
        mT = sb("mT", [2 * HEADS, 2, N], BF16)
        pT = sb("pT", [N, 2, HEADS, N])
        rden = sb("rden", [N, 2, HEADS]); a_sb = sb("a_sb", [N, 2, C])
        aT = sb("aT", [P, 2, CC, N])
        stats = sb("stats", [N, 3, 6]); mv = sb("mv", [N, 3, 2]); rstd = sb("rstd", [N, 3, 2])
        nmax = sb("nmax", [N, 2]); den = sb("den", [N, 2]); rdx = sb("rdx", [N, 2])

        with ExitStack() as early:
            def sbe(name, shape, dt=F32):
                return early.enter_context(nc.sbuf_tensor(name, shape, dt))
            qk = [sbe(f"qk{p}", [P, 2, 3 * CC, size * N], BF16) for p, size in enumerate(STACKS)]
            rest = sbe("rest", [P, 2, KT])
            wq = sbe("wq", [P, CC, C]); wk = sbe("wk", [P, CC, C])
            wv = sbe("wv", [P, CC, C]); xT_sb = sbe("xT_sb", [P, CC, NB * N])
        y = sb("y", [N, 3, C])
        x1 = sb("x1", [N, 3, C]); x1T = sb("x1T", [P, 2, CC, N])
        pv = sb("pv", [P, 2, 4 * N])
        px = sb("px", [N, 2, S]); pxT = sb("pxT", [SP_, 2, SC, N])
        x2 = sb("x2", [N, NB, C])
        x2h = sb("x2h", [P, CC, NB * N], F16); x2l = sb("x2l", [P, CC, NB * N], F16)
        h = sb("h", [P, HR, FT])
        o_sb = sb("o_sb", [N, 2, C])
        early_bytes = 4 * (CC * NB * N + 3 * CC * C + 2 * KT) + 3 * 2 * 2 * CC * NB * N
        late_bytes = 4 * (2 * 4 * N + 3 * C + 3 * C + 2 * CC * N + 2 * S + 2 * SC * N + NB * C + HR * FT + 2 * C) \
            + 2 * 2 * CC * NB * N
        sb("gap", [P, max(early_bytes - late_bytes, 4) // 4 + 16])

        qs = [sb(f"qs{p}", [GROUPS * D, HEADS, size * N], BF16) for p, size in enumerate(STACKS)]
        ks = [sb(f"ks{p}", [GROUPS * D, HEADS, size * N], BF16) for p, size in enumerate(STACKS)]

        with ExitStack() as weights:
            w1 = weights.enter_context(nc.sbuf_tensor("w1", [P, CC * FF], F32))
            w2 = weights.enter_context(nc.sbuf_tensor("w2", [P, FC * C], F32))
            wtmp = weights.enter_context(nc.sbuf_tensor("wtmp", [P, CC * FF], F32))
        hh = sb("hh", [P, FC, FT], F32R); hl = sb("hl", [P, FC, FT], F32R)
        sb("weights_end", [P, 3 * CC * FF - 2 * FC * FT])

        parts = [nc.dram_tensor(f"parts{p}", (2, 3, D * HEADS, size * N), BF16, kind="Internal").ap()
                 for p, size in enumerate(STACKS)]

        banks = ctx_.enter_context(nc.psum_tensor("banks", [P, 8, BANK], F32))
        bank_s = [0, 1]
        bank_t = [2, 3]
        bank_tp = [4, 5]
        bank_mm = [6, 7]

        in_wq = sem("in_wq"); in_wk = sem("in_wk"); in_wv = sem("in_wv")
        in_xT = [sem(f"in_xT{p}") for p in range(len(STACKS))]
        in_ffn = sem("in_ffn"); in_x = sem("in_x"); in_wo = sem("in_wo")
        in_b1 = sem("in_b1")
        in_ctxT = [sem(f"in_ctxT{b}") for b in range(NB)]; in_ctx = [sem(f"in_ctx{b}") for b in range(NB)]
        ones_ready = sem("ones_ready"); const_ready = sem("const_ready"); const_step = sem("const_step")
        proj_done = sem("proj_done"); part1_done = sem("part1_done"); rest_done = sem("rest_done")
        part2_done = sem("part2_done"); part3_done = sem("part3_done")
        parted = [[sem(f"parted_{side}{p}") for side in "qk"] for p in range(len(STACKS))]
        sel_done = sem("sel_done")
        stacked = [sem(f"stacked{p}") for p in range(len(STACKS))]
        v_kept = sem("v_kept")
        wsum_done = sem("wsum_done"); thr_done = sem("thr_done")
        tern_step = sem("tern_step"); tern_done = sem("tern_done")
        xb_done = sem("xb_done")
        s_done = sem("s_done"); max_done = sem("max_done"); mcat_step = sem("mcat_step")
        mcat_done = sem("mcat_done")
        t_done = sem("t_done"); exp_done = sem("exp_done"); pv_kept = sem("pv_kept")
        rden_done = sem("rden_done")
        turned = sem("turned")
        tp_free = [sem("tp_free0"), sem("tp_free1")]
        mm_done = sem("mm_done")
        x2h_done = sem("x2h_done")
        y_done = sem("y_done"); bn_done = sem("bn_done"); var_done = sem("var_done")
        eps_done = sem("eps_done"); rstd_done = sem("rstd_done"); ln_done = sem("ln_done")
        nmax_done = sem("nmax_done"); px_done = sem("px_done"); rdx_done = sem("rdx_done")
        x2b_done = sem("x2b_done")
        hid_done = sem("hid_done"); gelu_done = sem("gelu_done"); hh_done = sem("hh_done"); hl_done = [sem("hl_done0"), sem("hl_done1")]
        stored = [sem("stored0"), sem("stored1")]

        block = ctx_.enter_context(nc.Block())

        TURNS = [st for st in ORDER if st[0] in "MWXACEG"]
        RESULTS = [st for st in ORDER if st[0] in "UVBDFI"]
        SUMS = [st for st in ORDER if st[0] in "BFI"]
        ENDS = [st for st in ORDER if st[0] in ("L1", "L2", "L3")]

        SUM_OF = {"L1": "B", "L2": "F", "L3": "I"}
        END_OF = {s: l for l, s in SUM_OF.items()}

        def count(uses, stage, b):
            return uses.index((stage, b)) + 1

        def tp_of(stage, b):
            return banks[:, bank_tp[(count(TURNS, stage, b) - 1) % 2], :]

        def bank_of(stage, b):
            return (count(RESULTS, stage, b) - 1) % 2

        def piece(n):
            width = 2 * CC * FF // PIECES
            n %= PIECES // 2
            return slice(n * width, (n + 1) * width)

        def tp_read(eng, stage, b):
            use = count(TURNS, stage, b)
            eng.wait_ge(tp_free[(use - 1) % 2], (use + 1) // 2)

        def tp_freed(stage, b):
            return tp_free[(count(TURNS, stage, b) - 1) % 2]

        def quads(stage):
            return range(QUADS // 2) if stage[1] == "a" else range(QUADS // 2, QUADS)

        def cols(b):
            return slice(b * N, (b + 1) * N)

        def piece_cols(p):
            return slice(START[p] * N, START[p + 1] * N)

        def in_stack(stack, head, b):
            p = sum(b >= start for start in START[1:])
            return stack[p][:, head, (b - START[p]) * N:(b - START[p] + 1) * N]

        def parts_gone(eng):
            for p in range(len(STACKS)):
                for side in range(2):
                    eng.wait_ge(parted[p][side], 16)

        @block.sync
        def _(sp):
            xv = xT.rearrange("(c p) n -> p c n", p=P)
            sp.dma_start(wq[:, :, :], WqT.rearrange("(c p) n -> p c n", p=P)).then_inc(in_wq, 16)
            sp.dma_start(xT_sb[:, :, piece_cols(0)], xv[:, :, piece_cols(0)]).then_inc(in_xT[0], 16)
            sp.dma_start(wk[:, :, :], WkT.rearrange("(c p) n -> p c n", p=P)).then_inc(in_wk, 16)
            sp.dma_start(xT_sb[:, :, piece_cols(1)], xv[:, :, piece_cols(1)]).then_inc(in_xT[1], 16)
            sp.dma_start(wv[:, :, :], WvT.rearrange("(c p) n -> p c n", p=P)).then_inc(in_wv, 16)
            for p in range(2, len(STACKS)):
                sp.dma_start(xT_sb[:, :, piece_cols(p)], xv[:, :, piece_cols(p)]).then_inc(in_xT[p], 16)

            def write_parts(p):
                for side in range(2):
                    sp.wait_ge(part3_done, CC * (2 * p + side + 1))
                    sp.dma_start(parts[p][side].rearrange("r (c p) n -> p (r c) n", p=P),
                                 qk[p][:, side, :, :]).then_inc(parted[p][side], 16)

            def read_stack(p):
                for side, (dst, runs) in enumerate(((qs[p], Q_RUNS), (ks[p], K_RUNS))):
                    sp.wait_ge(parted[p][side], 16)
                    rows = parts[p][side].rearrange("r (d h) n -> (r d) h n", d=D)
                    for group, part, length in runs:
                        sp.dma_start(dst[group * D:(group + length) * D, :, :],
                                     rows[part * D:(part + length) * D, :, :]).then_inc(stacked[p], 16)

            def load_context(b):
                if b >= CR:
                    sp.wait_ge(mm_done, count(RESULTS, "F", b - CR))
                sp.dma_start(ctxT_sb[:, :, b % CR, :],
                             ctxT[b].rearrange("(c p) s -> p c s", p=P)).then_inc(in_ctxT[b], 16)
                sp.dma_start(ctx_sb[:, :, b % CR, :],
                             ctx[b].rearrange("(c p) n -> p c n", p=SP_)).then_inc(in_ctx[b], 16)

            for stage, b in ORDER:
                if stage == "K":
                    write_parts(b)
                if stage == "R":
                    read_stack(b)
                if stage == "Load" and b == 0:
                        sp.dma_start(wo[:, :, :], WoT.rearrange("(c p) n -> p c n", p=P)).then_inc(in_wo, 16)
                        sp.dma_start(x_sb[:, :, :], x.rearrange("b n c -> n b c")).then_inc(in_x, 16)
                        sp.dma_start(bo_bc[:, :], bo.partition_broadcast(N)).then_inc(in_x, 16)
                        sp.dma_start(b2_bc[:, :], b2.partition_broadcast(N)).then_inc(in_x, 16)
                        sp.dma_start(b1_sb[:, :], b1).then_inc(in_b1, 16)
                if stage == "J":
                    load_context(b)
                if stage == "Load" and b == 1:
                    sp.dma_start(w1[:, :].rearrange("p (c f) -> p c f", c=CC),
                                 W1T.rearrange("(c p) f -> p c f", p=P)).then_inc(in_ffn, 16)
                    sp.dma_start(w2[:, :].rearrange("p (c n) -> p c n", c=FC),
                                 W2T.rearrange("(c p) n -> p c n", p=P)).then_inc(in_ffn, 16)
                if stage == "L3":
                    sp.wait_ge(ln_done, count(ENDS, "L3", b))
                    sp.dma_start(out[b], o_sb[:, b % 2, :]).then_inc(stored[b % 2], 16)
            for k in range(2):
                sp.wait_ge(stored[k], 16 * (NB // 2))

        @block.gpsimd
        def _(pool):
            pool.memset(ones[:, :], 1.0).then_inc(ones_ready, 1)
            pool.memset(half_neg[:, :], -0.5).then_inc(const_ready, 1)
            pool.memset(identf[:, :], 0.0).then_inc(const_step, 1)
            pool.memset(identb[:, :], 0.0).then_inc(const_step, 1)
            pool.wait_ge(const_step, 2)
            for ident in (identf, identb):
                pool.affine_select(out=ident[:, :], in_=ident[:, :], compare_op=ALU.not_equal, fill=1.0,
                                   base=0, pattern=[[-1, P]], channel_multiplier=1).then_inc(const_ready, 1)
            pool.memset(sel[:, :, :], 0.0).then_inc(sel_done, 1)
            for r in range(2):
                pool.wait_ge(sel_done, r + 1)
                pool.affine_select(out=sel[:, :, :], in_=sel[:, :, :], compare_op=ALU.not_equal, fill=-1.0,
                                   base=-r * HEADS, pattern=[[-1, HEADS], [0, N]],
                                   channel_multiplier=1).then_inc(sel_done, 1)
            pool.wait_ge(sel_done, 3)
            pool.memset(v_sb[:, :, :, D:], 0.0).then_inc(const_step, 1)
            pool.wait_ge(const_step, 3)
            pool.memset(v_sb[:, :, :, D:D + 1], 1.0).then_inc(const_ready, 1)

            pool.wait_ge(in_x, 48)
            pool.tensor_tensor(x_sb[:, :, :], x_sb[:, :, :],
                               bo_bc[:, :].unsqueeze(1).broadcast_to((N, NB, C)), ALU.add).then_inc(xb_done, 1)

            sums = 0
            for stage, b in ORDER:
                if stage in ("B", "F", "I"):
                    k = sums % 3
                    sums += 1
                    pool.wait_ge(var_done, sums)
                    pool.tensor_scalar(rstd[:, k, 0:1], mv[:, k, 1:2], EPS, None, ALU.add).then_inc(eps_done, 1)
                    pool.wait_ge(eps_done, sums)
                    pool.tensor_tensor(rstd[:, k, 1:2], rstd[:, k, 0:1], half_neg[0:N, :],
                                       ALU.pow).then_inc(rstd_done, 1)
                if stage == "H" and b % 2 == 1:
                    g, f = b // FC, b % FC
                    tokens = FFN[g] * N
                    pool.wait_ge(hh_done, b + 1)
                    pool.tensor_tensor(hl[:, f, 0:tokens], h[:, b % HR, 0:tokens],
                                       hh[:, f, 0:tokens].bitcast(F32), ALU.subtract).then_inc(hl_done[1], 1)
                if stage == "G":
                    pool.wait_ge(turned, count(TURNS, "G", b))
                    pool.tensor_tensor(x2[:, b, :], x2[:, b, :], b2_bc[:, :], ALU.add).then_inc(x2b_done, 1)

        @block.scalar
        def _(act):
            def part2(p, i):
                side, c, n = i // CC, i % CC, 2 * CC * p + i
                act.wait_ge(rest_done, n + 1)
                act.activation(qk[p][:, side, CC + c, :], rest[:, n % 2, 0:STACKS[p] * N],
                               ACT.Copy).then_inc(part2_done, 1)

            for stage, b in ORDER:
                if stage == "K":
                    for i in range(2 * CC):
                        n = 2 * CC * b + i
                        act.wait_ge(proj_done, n + 1)
                        act.activation(qk[b][:, i // CC, i % CC, :],
                                       banks[:, n % 4, 0:STACKS[b] * N], ACT.Copy).then_inc(part1_done, 1)
                        if i:
                            part2(b, i - 1)
                    part2(b, 2 * CC - 1)
                if stage == "U":
                    if b == 0:
                        act.wait_ge(const_ready, 4)
                    act.wait_ge(mm_done, count(RESULTS, "U", b))
                    act.activation(v_sb[:, b, :, 0:D],
                                   banks[0:N, bank_mm[bank_of("U", b)], 0:C].rearrange("n (h d) -> n h d", d=D),
                                   ACT.Copy).then_inc(v_kept, 1)
                if stage == "Z":
                    act.wait_ge(in_ffn, 32)
                    if b:
                        act.wait_ge(wsum_done, 1)
                    act.activation(wtmp[:, :], (w1, w2)[b][:, :], ACT.Abs,
                                   accum_out=wsum[:, b:b + 1]).then_inc(wsum_done, 1)
                if stage in ("Ta", "Tb"):
                    for q in quads(stage):
                        n = QUADS * b + q
                        act.wait_ge(t_done, n + 1)
                        if b >= 2:
                            act.wait_ge(mm_done, count(RESULTS, "V", b - 2))
                        act.activation(pT[:, b % 2, 4 * q:4 * q + 4, :],
                                       banks[0:N, bank_t[n % 2], 0:4 * N].rearrange("k (h n) -> k h n", n=N),
                                       ACT.Exp, scale=float(D) ** -0.5).then_inc(exp_done, 1)
                if stage == "V":
                    act.wait_ge(mm_done, count(RESULTS, "V", b))
                    if b == 0:
                        parts_gone(act)
                    if b >= 2:
                        act.wait_ge(turned, count(TURNS, "W", b - 2))
                    act.activation(pv[:, b % 2, :], banks[:, bank_mm[bank_of("V", b)], 0:4 * N], ACT.Copy).then_inc(pv_kept, 1)
                if stage in ("A", "C"):
                    use = count(TURNS, stage, b)
                    act.wait_ge(turned, use)
                    if b >= 2:
                        act.wait_ge(mm_done, count(RESULTS, "B" if stage == "A" else "D", b - 2))
                    act.activation((aT if stage == "A" else x1T)[:, b % 2, :, :],
                                   tp_of(stage, b)[:, 0:CC * N].rearrange("p (c n) -> p c n", n=N),
                                   ACT.Copy).then_inc(tp_freed(stage, b), 1)
                if stage == "D":
                    act.wait_ge(nmax_done, b + 1)
                    if b >= 2:
                        act.wait_ge(turned, count(TURNS, "E", b - 2))
                        act.wait_ge(rdx_done, b - 1)
                    act.activation(px[:, b % 2, :], banks[0:N, bank_mm[bank_of("D", b)], 0:S], ACT.Exp,
                                   bias=nmax[:, b % 2:b % 2 + 1],
                                   accum_out=den[:, b % 2:b % 2 + 1]).then_inc(px_done, 1)
                if stage == "E":
                    act.wait_ge(turned, count(TURNS, "E", b))
                    if b >= 2:
                        act.wait_ge(mm_done, count(RESULTS, "F", b - 2))
                    act.activation(pxT[:, b % 2, :, :],
                                   tp_of(stage, b)[0:SP_, 0:SC * N].rearrange("p (c n) -> p c n", n=N),
                                   ACT.Copy).then_inc(tp_freed(stage, b), 1)
                if stage == "G":
                    act.wait_ge(turned, count(TURNS, "G", b))
                    if b == 0:
                        act.wait_ge(mm_done, count(RESULTS, "U", NB - 1))
                    act.activation(x2h[:, :, cols(b)],
                                   tp_of(stage, b)[:, 0:CC * N].rearrange("p (c n) -> p c n", n=N),
                                   ACT.Copy).then_inc(x2h_done, 1)
                if stage == "H":
                    if b == 0:
                        act.wait_ge(in_b1, 16)
                    act.wait_ge(hid_done, b + 1)
                    if b >= HR:
                        act.wait_ge(hl_done[b % 2], (b - HR) // 2 + 1)
                    tokens = FFN[b // FC] * N
                    bank = bank_s[b % 2] if b < FC else (bank_s + bank_t)[b % 4]
                    act.activation(h[:, b % HR, 0:tokens], banks[:, bank, 0:tokens], ACT.Gelu,
                                   bias=b1_sb[:, b % FC:b % FC + 1]).then_inc(gelu_done, 1)

        @block.vector
        def _(dve):
            def part3(p, i):
                side, c, n = i // CC, i % CC, 2 * CC * p + i
                dve.wait_ge(part2_done, n + 1)
                dve.tensor_tensor(qk[p][:, side, 2 * CC + c, :], rest[:, n % 2, 0:STACKS[p] * N],
                                  qk[p][:, side, CC + c, :], ALU.subtract).then_inc(part3_done, 1)

            sums = 0

            def statistics(k):
                dve.wait_ge(y_done, sums)
                dve.bn_stats(stats[:, k, :], y[:, k, :]).then_inc(bn_done, 1)
                dve.wait_ge(bn_done, sums)
                dve.bn_aggr(mv[:, k, :], stats[:, k, :]).then_inc(var_done, 1)

            for stage, b in ORDER:
                if stage == "K":
                    for i in range(2 * CC):
                        n = 2 * CC * b + i
                        dve.wait_ge(part1_done, n + 1)
                        if n >= 2:
                            dve.wait_ge(part3_done, n - 1)
                        dve.tensor_tensor(rest[:, n % 2, 0:STACKS[b] * N], banks[:, n % 4, 0:STACKS[b] * N],
                                          qk[b][:, i // CC, i % CC, :],
                                          ALU.subtract).then_inc(rest_done, 1)
                        if i:
                            part3(b, i - 1)
                    part3(b, 2 * CC - 1)
                if stage == "X":
                    dve.wait_ge(turned, count(TURNS, "X", 0))
                    dve.tensor_scalar(thr[:, 4:6], tp_of(stage, b)[:, 0:2], 1.0 / (C * FF), 1e-8,
                                      ALU.mult, ALU.max).then_inc(tp_freed(stage, b), 1)
                    tp_read(dve, "X", 0)
                    dve.tensor_scalar(thr[:, 0:2], thr[:, 4:6], 0.5, None, ALU.mult).then_inc(thr_done, 1)
                    dve.tensor_scalar(thr[:, 2:4], thr[:, 4:6], -0.5, None, ALU.mult).then_inc(thr_done, 1)
                if stage == "Y":
                    if b == 0:
                        dve.wait_ge(thr_done, 2)
                    n, cs = b // (PIECES // 2), piece(b)
                    w, t = (w1, t1) if n == 0 else (w2, t2)
                    if n:
                        dve.wait_ge(tern_done, b - PIECES // 2 + 1)
                    dve.tensor_scalar(wtmp[:, cs], w[:, cs], thr[:, 2 + n:3 + n], None,
                                      ALU.is_lt).then_inc(tern_step, 1)
                    dve.wait_ge(tern_step, b + 1)
                    dve.scalar_tensor_tensor(t[:, :, :].rearrange("p c n -> p (c n)")[:, cs], w[:, cs],
                                             thr[:, n:n + 1], wtmp[:, cs], ALU.is_gt,
                                             ALU.subtract).then_inc(tern_done, 1)
                if stage in ("Sa", "Sb"):
                    if b >= 2:
                        dve.wait_ge(mcat_done, b - 1)
                    for q in quads(stage):
                        n = QUADS * b + q
                        dve.wait_ge(s_done, n + 1)
                        dve.tensor_reduce(mx[:, b % 2, 4 * q:4 * q + 4],
                                          banks[0:N, bank_s[n % 2], 0:4 * N].rearrange("q (h k) -> q h k", k=N),
                                          AX.X, ALU.max).then_inc(max_done, 1)
                if stage == "Sb":
                    dve.wait_ge(max_done, QUADS * (b + 1))
                    dve.tensor_copy(mcat[:, b % 2, 0:HEADS], mx[:, b % 2, :]).then_inc(mcat_step, 1)
                    dve.wait_ge(mcat_step, b + 1)
                    dve.tensor_tensor(mcat[:, b % 2, HEADS:2 * HEADS], mx[:, b % 2, :],
                                      mcat[:, b % 2, 0:HEADS], ALU.subtract).then_inc(mcat_done, 1)
                if stage == "M":
                    dve.wait_ge(turned, count(TURNS, "M", b))
                    if b >= 2:
                        dve.wait_ge(t_done, QUADS * (b - 1))
                    dve.tensor_copy(mT[:, b % 2, :],
                                    tp_of(stage, b)[0:2 * HEADS, 0:N // 2].bitcast(BF16)).then_inc(tp_freed(stage, b), 1)
                if stage == "W":
                    av = tp_of(stage, b)[0:N, :].rearrange("n (h e) -> n h e", e=32)
                    dve.wait_ge(turned, count(TURNS, "W", b))
                    if b >= 2:
                        tp_read(dve, "W", b - 2)
                    dve.reciprocal(rden[:, b % 2, :], av[:, :, D]).then_inc(rden_done, 1)
                    if b >= 2:
                        dve.wait_ge(turned, count(TURNS, "A", b - 2))
                    dve.wait_ge(rden_done, b + 1)
                    dve.tensor_tensor(a_sb[:, b % 2, :].rearrange("n (h d) -> n h d", d=D), av[:, :, 0:D],
                                      rden[:, b % 2, :].unsqueeze(2).broadcast_to((N, HEADS, D)),
                                      ALU.mult).then_inc(tp_freed(stage, b), 1)
                if stage == "D":
                    dve.wait_ge(mm_done, count(RESULTS, "D", b))
                    if b >= 2:
                        dve.wait_ge(px_done, b - 1)
                    dve.tensor_reduce(nmax[:, b % 2:b % 2 + 1], banks[0:N, bank_mm[bank_of("D", b)], 0:S],
                                      AX.X, ALU.max, negate=True).then_inc(nmax_done, 1)
                if stage == "E":
                    dve.wait_ge(px_done, b + 1)
                    dve.reciprocal(rdx[:, b % 2:b % 2 + 1], den[:, b % 2:b % 2 + 1]).then_inc(rdx_done, 1)
                if stage in ("B", "F", "I"):
                    k = sums % 3
                    sums += 1
                    bank = bank_of(stage, b)
                    if sums == 1:
                        parts_gone(dve)
                    dve.wait_ge(mm_done, count(RESULTS, stage, b))
                    psum = banks[0:N, bank_mm[bank], 0:C]
                    if sums > 3:
                        dve.wait_ge(ln_done, count(ENDS, END_OF[SUMS[sums - 4][0]], SUMS[sums - 4][1]))
                    if stage == "B":
                        if b == 0:
                            dve.wait_ge(xb_done, 1)
                        dve.tensor_tensor(y[:, k, :], psum, x_sb[:, b, :], ALU.add).then_inc(y_done, 1)
                    if stage == "F":
                        dve.wait_ge(rdx_done, b + 1)
                        dve.scalar_tensor_tensor(y[:, k, :], psum, rdx[:, b % 2:b % 2 + 1], x1[:, b % 3, :],
                                                 ALU.mult, ALU.add).then_inc(y_done, 1)
                    if stage == "I":
                        dve.wait_ge(x2b_done, b + 1)
                        dve.tensor_tensor(y[:, k, :], psum, x2[:, b, :], ALU.add).then_inc(y_done, 1)
                    statistics(k)
                if stage in ("L1", "L2", "L3"):
                    use = count(SUMS, SUM_OF[stage], b)
                    k = (use - 1) % 3
                    dve.wait_ge(rstd_done, use)
                    if stage == "L1":
                        if b >= 3:
                            dve.wait_ge(turned, count(TURNS, "C", b - 3))
                        to = x1[:, b % 3, :]
                    if stage == "L2":
                        to = x2[:, b, :]
                    if stage == "L3":
                        if b >= 2:
                            dve.wait_ge(stored[b % 2], 16 * (b // 2))
                        to = o_sb[:, b % 2, :]
                    dve.tensor_scalar(to, y[:, k, :], mv[:, k, 0:1], rstd[:, k, 1:2], ALU.subtract,
                                      ALU.mult).then_inc(ln_done, 1)
                if stage == "G":
                    dve.wait_ge(x2h_done, b + 1)
                    if b == 0:
                        dve.wait_ge(mm_done, count(RESULTS, "U", NB - 1))
                    dve.tensor_tensor(x2l[:, :, cols(b)],
                                      tp_of(stage, b)[:, 0:CC * N].rearrange("p (c n) -> p c n", n=N),
                                      x2h[:, :, cols(b)], ALU.subtract).then_inc(tp_freed(stage, b), 1)
                if stage == "H":
                    g, f = b // FC, b % FC
                    tokens = FFN[g] * N
                    if b == 0:
                        dve.wait_ge(tern_done, PIECES)
                    elif f == 0:
                        dve.wait_ge(mm_done, count(RESULTS, "I", FIRST[g] - 1))
                    dve.wait_ge(gelu_done, b + 1)
                    dve.tensor_copy(hh[:, f, 0:tokens], h[:, b % HR, 0:tokens]).then_inc(hh_done, 1)
                    if f % 2 == 0:
                        dve.wait_ge(hh_done, b + 1)
                        dve.tensor_tensor(hl[:, f, 0:tokens], h[:, b % HR, 0:tokens],
                                          hh[:, f, 0:tokens].bitcast(F32), ALU.subtract).then_inc(hl_done[0], 1)

        @block.tensor
        def _(pe):
            def bank_tp_ready(stage, b):
                use = count(TURNS, stage, b)
                if use > 2:
                    pe.wait_ge(tp_free[(use - 1) % 2], (use - 1) // 2)

            def bank_mm_ready(stage, b):
                use = count(RESULTS, stage, b)
                if use > 2:
                    last, lb = RESULTS[use - 3]
                    if last == "D":
                        pe.wait_ge(px_done, lb + 1)
                    elif last == "U":
                        pe.wait_ge(v_kept, lb + 1)
                    elif last == "V":
                        pe.wait_ge(pv_kept, lb + 1)
                    else:
                        pe.wait_ge(y_done, count(SUMS, last, lb))
                return banks[0:N, bank_mm[(use - 1) % 2], :]

            def turn(to, src, rows, parts):
                for c in range(parts):
                    w = src.shape[1] // parts
                    mm = pe.transpose(to[0:w, c * rows:(c + 1) * rows],
                                      src[:, c * w:(c + 1) * w], identf[0:rows, 0:rows])
                mm.then_inc(turned, 1)

            pe.wait_ge(ones_ready, 1)
            for _ in range(WARM_UP):
                pe.matmul(banks[:, bank_t[1], 0:P], ones[:, :], ones[:, :], start=True, stop=True)

            for stage, b in ORDER:
                if stage == "K":
                    pe.wait_ge(in_xT[b], 16)
                    for i in range(2 * CC):
                        n = 2 * CC * b + i
                        w, m = (wq, wk)[i // CC], i % CC
                        if b == 0 and m == 0:
                            pe.wait_ge((in_wq, in_wk)[i // CC], 16)
                        if n >= 4:
                            pe.wait_ge(rest_done, n - 3)
                        for c in range(CC):
                            mm = pe.matmul(banks[:, n % 4, 0:STACKS[b] * N], w[:, c, m * P:(m + 1) * P],
                                           xT_sb[:, c, piece_cols(b)], start=(c == 0), stop=(c == CC - 1))
                        mm.then_inc(proj_done, 1)
                if stage == "U":
                    if b == 0:
                        pe.wait_ge(in_wv, 16)
                    to = bank_mm_ready("U", b)
                    for c in range(CC):
                        mm = pe.matmul(to[:, 0:C], xT_sb[:, c, cols(b)], wv[:, c, :],
                                       start=(c == 0), stop=(c == CC - 1))
                    mm.then_inc(mm_done, 1)
                if stage == "X":
                    pe.wait_ge(wsum_done, 2)
                    bank_tp_ready("X", 0)
                    pe.matmul(tp_of(stage, b)[:, 0:2], ones[:, :], wsum[:, 0:2],
                              start=True, stop=True).then_inc(turned, 1)
                if stage in ("Sa", "Sb"):
                    if stage == "Sa" and b == 0:
                        pe.wait_ge(const_ready, 4)
                        pe.wait_ge(rest_done, 2 * CC * len(STACKS))
                    if stage == "Sa" and b in START:
                        pe.wait_ge(stacked[START.index(b)], 16 * (len(Q_RUNS) + len(K_RUNS)))
                    for q in quads(stage):
                        n = QUADS * b + q
                        if n >= 2:
                            pe.wait_ge(max_done, n - 1)
                        for j in range(4):
                            mm = pe.matmul(banks[0:N, bank_s[n % 2], j * N:(j + 1) * N],
                                           in_stack(qs, 4 * q + j, b), in_stack(ks, 4 * q + j, b),
                                           start=True, stop=True)
                        mm.then_inc(s_done, 1)
                if stage == "M":
                    pe.wait_ge(mcat_done, b + 1)
                    bank_tp_ready("M", b)
                    pe.transpose(tp_of(stage, b)[0:2 * HEADS, 0:N // 2].bitcast(BF16), mcat[:, b % 2, :],
                                 identb[0:N, 0:N]).then_inc(turned, 1)
                if stage in ("Ta", "Tb"):
                    if b == 0:
                        pe.wait_ge(sel_done, 3)
                    tp_read(pe, "M", b)
                    for q in quads(stage):
                        n = QUADS * b + q
                        if n >= 2:
                            pe.wait_ge(exp_done, n - 1)
                        for j in range(4):
                            to = banks[0:N, bank_t[n % 2], j * N:(j + 1) * N]
                            pe.matmul(to, in_stack(ks, 4 * q + j, b), in_stack(qs, 4 * q + j, b),
                                      start=True, stop=False)
                            mm = pe.matmul(to, sel[:, 4 * q + j, :], mT[:, b % 2, :],
                                           start=False, stop=True)
                        mm.then_inc(t_done, 1)
                if stage == "V":
                    pe.wait_ge(exp_done, QUADS * (b + 1))
                    pe.wait_ge(v_kept, b + 1)
                    bank_mm_ready("V", b)
                    for hd in range(HEADS):
                        r, j = hd // 4, hd % 4
                        mm = pe.matmul(banks[32 * j:32 * j + 32, bank_mm[bank_of("V", b)], r * N:(r + 1) * N],
                                       v_sb[:, b, hd, :], pT[:, b % 2, hd, :], start=True, stop=True)
                    mm.then_inc(mm_done, 1)
                if stage == "W":
                    pe.wait_ge(pv_kept, b + 1)
                    bank_tp_ready("W", b)
                    for r in range(HEADS // 4):
                        mm = pe.transpose(tp_of(stage, b)[0:N, r * P:(r + 1) * P],
                                          pv[:, b % 2, r * N:(r + 1) * N], identf[:, :])
                    mm.then_inc(turned, 1)
                if stage == "A":
                    tp_read(pe, "W", b)
                    bank_tp_ready("A", b)
                    turn(tp_of(stage, b), a_sb[:, b % 2, :], N, CC)
                if stage == "B":
                    tp_read(pe, "A", b)
                    if b == 0:
                        pe.wait_ge(in_wo, 16)
                    to = bank_mm_ready("B", b)
                    for c in range(CC):
                        mm = pe.matmul(to[:, 0:C], aT[:, b % 2, c, :], wo[:, c, :],
                                       start=(c == 0), stop=(c == CC - 1))
                    mm.then_inc(mm_done, 1)
                if stage == "C":
                    pe.wait_ge(ln_done, count(ENDS, "L1", b))
                    bank_tp_ready("C", b)
                    turn(tp_of(stage, b), x1[:, b % 3, :], N, CC)
                if stage == "D":
                    tp_read(pe, "C", b)
                    pe.wait_ge(in_ctxT[b], 16)
                    to = bank_mm_ready("D", b)
                    for c in range(CC):
                        mm = pe.matmul(to[:, 0:S], x1T[:, b % 2, c, :], ctxT_sb[:, c, b % CR, :],
                                       start=(c == 0), stop=(c == CC - 1))
                    mm.then_inc(mm_done, 1)
                if stage == "E":
                    pe.wait_ge(px_done, b + 1)
                    bank_tp_ready("E", b)
                    turn(tp_of(stage, b), px[:, b % 2, :], N, SC)
                if stage == "F":
                    tp_read(pe, "E", b)
                    pe.wait_ge(in_ctx[b], 16)
                    to = bank_mm_ready("F", b)
                    for c in range(SC):
                        mm = pe.matmul(to[:, 0:C], pxT[:, b % 2, c, :], ctx_sb[:, c, b % CR, :],
                                       start=(c == 0), stop=(c == SC - 1))
                    mm.then_inc(mm_done, 1)
                if stage == "G":
                    pe.wait_ge(ln_done, count(ENDS, "L2", b))
                    bank_tp_ready("G", b)
                    turn(tp_of(stage, b), x2[:, b, :], N, CC)
                if stage == "H":
                    g, f = b // FC, b % FC
                    if b == 0:
                        pe.wait_ge(max_done, QUADS * NB)
                        pe.wait_ge(tern_done, PIECES // 2)
                    tp_read(pe, "G", FIRST[g + 1] - 1)
                    bank = banks[:, bank_s[b % 2] if g == 0 else (bank_s + bank_t)[b % 4], :]
                    if b == FC:
                        pe.wait_ge(exp_done, QUADS * NB)
                    if b >= 2:
                        pe.wait_ge(gelu_done, b - 1 if b < FC + 2 else b - 3)
                    mms = [(c, part) for c in range(CC) for part in (x2h, x2l)]
                    for i, (c, part) in enumerate(mms):
                        mm = pe.matmul(bank[:, 0:FFN[g] * N], t1[:, c, f * P:(f + 1) * P],
                                       part[:, c, FIRST[g] * N:FIRST[g + 1] * N],
                                       start=(i == 0), stop=(i == len(mms) - 1))
                    mm.then_inc(hid_done, 1)
                if stage == "I":
                    to = bank_mm_ready("I", b)
                    if b == 0:
                        pe.wait_ge(tern_done, PIECES)
                    mms = [(f, part) for f in range(FC) for part in (hh, hl)]
                    for i, (f, part) in enumerate(mms):
                        g = GROUP_OF[b]
                        if b == FIRST[g]:
                            pe.wait_ge(hl_done[f % 2], (FC * g + f) // 2 + 1)
                        mm = pe.matmul(to[:, 0:C], part[:, f, cols(b - FIRST[g])], t2[:, f, :],
                                       start=(i == 0), stop=(i == len(mms) - 1))
                    mm.then_inc(mm_done, 1)

    return nc


def kernel(**inputs):
    import numpy as np
    import concourse.bacc as bacc
    from concourse.bass_utils import run_bass_kernel_spmd

    a = {k: np.asarray(v) for k, v in inputs.items()}

    def turned(m):
        return np.ascontiguousarray(np.moveaxis(m, -1, -2))

    def by_depth(m):
        return np.moveaxis(m.reshape(HEADS, -1, m.shape[-1]), 0, 1).reshape(m.shape)

    x, ctx = a["x"], a["ctx_1024"]
    arrays = {
        "x": x,
        "xT": turned(x.reshape(-1, x.shape[-1])),
        "ctx": ctx,
        "ctxT": turned(ctx),
        "WqT": turned(by_depth(a["L0_attn_Wq"])), "WkT": turned(by_depth(a["L0_attn_Wk"])), "WvT": turned(a["L0_attn_Wv"]),
        "WoT": turned(a["L0_attn_Wout"]), "bo": a["L0_attn_bout"],
        "W1T": turned(a["L0_ffn_W1"]), "b1": turned(a["L0_ffn_b1"].reshape(-1, P)),
        "W2T": turned(a["L0_ffn_W2"]), "b2": a["L0_ffn_b2"],
    }
    arrays = {f"in_{k}": np.ascontiguousarray(v) for k, v in arrays.items()}
    nc = bacc.Bacc("TRN2", target_bir_lowering=False, num_devices=1)
    args = [nc.dram_tensor(k, v.shape, mybir.dt.from_np(v.dtype), kind="ExternalInput").ap()
            for k, v in arrays.items()]
    args.append(nc.dram_tensor("out", x.shape, F32, kind="ExternalOutput").ap())
    decoder_layer(nc, *args)
    r = run_bass_kernel_spmd(nc, [arrays], core_ids=[0])
    return r.results[0]["out"]
```

```python
from contextlib import ExitStack

import concourse.bass as bass
from concourse import mybir

F32 = mybir.dt.float32
F32R = mybir.dt.float32r
BF16 = mybir.dt.bfloat16
F16 = mybir.dt.float16
ALU = mybir.AluOpType
ACT = mybir.ActivationFunctionType
AX = mybir.AxisListType

P = 128
EPS = 1e-5
HEADS = 16
BANK = 512
GROUPS = 6
Q_RUNS = ((0, 0, 3), (3, 0, 2), (5, 0, 1))
K_RUNS = ((0, 0, 1), (1, 0, 1), (2, 0, 2), (4, 1, 2))
WARM_UP = 8
PIECES = 8
STACKS = (2, 3, 3)
FFN = (3, 2, 2, 1)

STEPS = """
K:0 Load:0 K:1 K:2 K:3 U:0 U:1 K:4 K:5 R:0 K:6 K:7 K:8 K:9 K:10
Sa:0 K:11 U:2 R:1 Sb:0 U:3 U:4 M:0 J:0
Sa:1 Ta:0 U:5 Load:1 R:2 Tb:0 Sb:1 V:0 M:1 U:6 W:0 U:7 A:0
Sa:2 Ta:1 Sb:2 Tb:1
Sa:3 M:2 B:0 V:1 Ta:2 L1:0 W:1 Sb:3 J:1 C:0 Tb:2 A:1 D:0 M:3
Sa:4 B:1 E:0 L1:1 Z:0 V:2 F:0 J:2 J:3 Ta:3 W:2 C:1 L2:0 Sb:4 A:2 Z:1 D:1 B:2 Tb:3 X:0 N:0
Sa:5 L1:2 E:1 N:1 G:0 V:3 N:2 M:4 Y:0 F:1 C:2 N:3 W:3 Ta:4 Y:1 Sb:5 Tb:4 A:3 D:2
Sa:6 J:4 L2:1 M:5 B:3 N:4 V:4 Y:2 E:2 Y:3 N:5 L1:3 Ta:5 G:1 W:4 F:2 C:3 Sb:6 Tb:5 A:4 D:3 M:6 Y:4 B:4
    N:6 L2:2
Sa:7 E:3 L1:4 V:5 Y:5 G:2 F:3 Ta:6 W:5 Sb:7 C:4 Tb:6 N:7 D:4 Y:6 L2:3 A:5 Y:7 H:0 J:5 J:6 H:1 V:6 E:4
    B:5 H:2 H:3 G:3 H:4 H:5 L1:5 M:7 J:7 F:4 H:6 H:7 Ta:7 W:6 L2:4 C:5 I:0 A:6 L3:0 I:1 Tb:7 G:4 B:6
    L3:1 D:5 I:2 H:8 E:5 V:7 L1:6 H:9 H:10 H:11 W:7 H:12 C:6 F:5 H:13 D:6 A:7 L2:5 G:5 L3:2 B:7 H:14 E:6
    H:15 L1:7 F:6 L2:6 C:7 I:3 D:7 I:4 L3:3 E:7 G:6 F:7 H:16 H:17 H:18 L2:7 H:19 H:20 H:21 G:7 H:22 H:23
    H:24 H:25 H:26 H:27 L3:4 I:5 H:28 H:29 H:30 L3:5 H:31 I:6 I:7 L3:6 L3:7
"""


def order(batches, chunks):
    steps = [(s.split(":")[0], int(s.split(":")[1])) for s in STEPS.split()]
    assert [b for s, b in steps if s == "B"] == list(range(batches))
    assert [b for s, b in steps if s == "H"] == list(range(chunks * len(FFN)))
    return steps


def decoder_layer(nc, x, xT, ctx, ctxT, WqT, WkT, WvT, WoT, bo, W1T, b1, W2T, b2, out):
    NB, N, C = x.shape
    S = ctx.shape[1]
    FF = W1T.shape[1]
    D = C // HEADS
    CC = C // P
    FC = FF // P
    SP_ = 125
    SC = S // SP_
    FT = max(FFN) * N
    KT = max(STACKS) * N
    FIRST = [sum(FFN[:g]) for g in range(len(FFN) + 1)]
    START = [sum(STACKS[:p]) for p in range(len(STACKS) + 1)]
    GROUP_OF = [g for g, size in enumerate(FFN) for _ in range(size)]
    HOME = [0] * (len(FFN) - 1) + [FFN[-2] * N]
    CR = 4
    HR = 4
    QUADS = HEADS // 4
    assert CC * P == C and SC * SP_ == S and GROUPS * D <= P and FIRST[-1] == START[-1] == NB
    assert max(FT, KT, 4 * N) <= BANK and NB <= 2 * CR
    ORDER = order(NB, FC)

    with ExitStack() as ctx_:
        def sb(name, shape, dt=F32):
            return ctx_.enter_context(nc.sbuf_tensor(name, shape, dt))

        def sem(name):
            return ctx_.enter_context(nc.semaphore(name))

        x_sb = sb("x_sb", [N, NB, C])
        wo = sb("wo", [P, CC, C])
        t1 = sb("t1", [P, CC, FF], F16)
        t2 = sb("t2", [P, FC, C], F32R)
        wsum = sb("wsum", [P, 2]); thr = sb("thr", [P, 6])
        bo_bc = sb("bo_bc", [N, C]); b2_bc = sb("b2_bc", [N, C])
        b1_sb = sb("b1_sb", [P, FC])
        ctx_sb = sb("ctx_sb", [SP_, SC, CR, C])
        ctxT_sb = sb("ctxT_sb", [P, CC, CR, S])
        ones = sb("ones", [P, P]); identf = sb("identf", [P, P])
        identb = sb("identb", [P, P], BF16)
        half_neg = sb("half_neg", [P, 1])
        v_sb = sb("v_sb", [N, NB, HEADS, 32])
        mx = sb("mx", [N, 2, HEADS]); mcat = sb("mcat", [N, 2, 2 * HEADS], BF16)
        sel = sb("sel", [2 * HEADS, HEADS, N], BF16)
        mT = sb("mT", [2 * HEADS, 2, N], BF16)
        pT = sb("pT", [N, 2, HEADS, N])
        rden = sb("rden", [N, 2, HEADS]); a_sb = sb("a_sb", [N, 2, C])
        aT = sb("aT", [P, 2, CC, N])
        stats = sb("stats", [N, 3, 6]); mv = sb("mv", [N, 3, 2]); rstd = sb("rstd", [N, 3, 2])
        nmax = sb("nmax", [N, 2]); den = sb("den", [N, 2]); rdx = sb("rdx", [N, 2])

        with ExitStack() as early:
            def sbe(name, shape, dt=F32):
                return early.enter_context(nc.sbuf_tensor(name, shape, dt))
            qk = [sbe(f"qk{p}", [P, 2, 3 * CC, size * N], BF16) for p, size in enumerate(STACKS)]
            rest = sbe("rest", [P, 2, KT])
            wq = sbe("wq", [P, CC, C]); wk = sbe("wk", [P, CC, C])
            wv = sbe("wv", [P, CC, C]); xT_sb = sbe("xT_sb", [P, CC, NB * N])
        y = sb("y", [N, 3, C])
        x1 = sb("x1", [N, 3, C]); x1T = sb("x1T", [P, 2, CC, N])
        pv = sb("pv", [P, 2, 4 * N])
        px = sb("px", [N, 2, S]); pxT = sb("pxT", [SP_, 2, SC, N])
        x2 = sb("x2", [N, NB, C])
        x2h = sb("x2h", [P, CC, NB * N], F16); x2l = sb("x2l", [P, CC, NB * N], F16)
        h = sb("h", [P, HR, FT])
        o_sb = sb("o_sb", [N, 2, C])
        early_bytes = 4 * (CC * NB * N + 3 * CC * C + 2 * KT) + 3 * 2 * 2 * CC * NB * N
        late_bytes = 2 * 2 * CC * NB * N + \
            4 * (8 * N + 6 * C + 2 * CC * N + 2 * S + 2 * SC * N + NB * C + HR * FT + 2 * C)
        sb("gap", [P, max(early_bytes - late_bytes, 4) // 4 + 16])

        qs = [sb(f"qs{p}", [GROUPS * D, HEADS, size * N], BF16) for p, size in enumerate(STACKS)]
        ks = [sb(f"ks{p}", [GROUPS * D, HEADS, size * N], BF16) for p, size in enumerate(STACKS)]

        with ExitStack() as weights:
            w1 = weights.enter_context(nc.sbuf_tensor("w1", [P, CC * FF], F32))
            w2 = weights.enter_context(nc.sbuf_tensor("w2", [P, FC * C], F32))
            wtmp = weights.enter_context(nc.sbuf_tensor("wtmp", [P, CC * FF], F32))
        hh = sb("hh", [P, FC, FT], F32R); hl = sb("hl", [P, FC, FT], F32R)
        sb("weights_end", [P, 3 * CC * FF - 2 * FC * FT])

        parts = [nc.dram_tensor(f"parts{p}", (2, 3, D * HEADS, size * N), BF16, kind="Internal").ap()
                 for p, size in enumerate(STACKS)]

        banks = ctx_.enter_context(nc.psum_tensor("banks", [P, 8, BANK], F32))
        bank_s = [0, 1]
        bank_t = [2, 3]
        bank_tp = [4, 5]
        bank_mm = [6, 7]

        in_wq = sem("in_wq"); in_wk = sem("in_wk"); in_wv = sem("in_wv")
        in_xT = [sem(f"in_xT{p}") for p in range(len(STACKS))]
        in_ffn = sem("in_ffn"); in_x = sem("in_x"); in_wo = sem("in_wo")
        in_b1 = sem("in_b1")
        in_ctxT = [sem(f"in_ctxT{b}") for b in range(NB)]; in_ctx = [sem(f"in_ctx{b}") for b in range(NB)]
        ones_ready = sem("ones_ready"); const_ready = sem("const_ready"); const_step = sem("const_step")
        part1_done = sem("part1_done"); rest_done = sem("rest_done")
        part2_done = sem("part2_done"); part3_done = sem("part3_done")
        parted = [[sem(f"parted_{side}{p}") for side in "qk"] for p in range(len(STACKS))]
        sel_done = sem("sel_done")
        stacked = [sem(f"stacked{p}") for p in range(len(STACKS))]
        v_kept = sem("v_kept")
        wsum_done = sem("wsum_done"); thr_done = sem("thr_done")
        tern_step = sem("tern_step"); tern_done = sem("tern_done")
        xb_done = sem("xb_done")
        s_done = sem("s_done"); max_done = sem("max_done"); mcat_step = sem("mcat_step")
        mcat_done = sem("mcat_done")
        t_done = sem("t_done"); exp_done = sem("exp_done"); pv_kept = sem("pv_kept")
        rden_done = sem("rden_done")
        turned = sem("turned")
        tp_free = [sem("tp_free0"), sem("tp_free1")]
        mm_done = sem("mm_done")
        x2h_done = sem("x2h_done")
        y_done = sem("y_done"); bn_done = sem("bn_done"); var_done = sem("var_done")
        eps_done = sem("eps_done"); rstd_done = sem("rstd_done"); ln_done = sem("ln_done")
        nmax_done = sem("nmax_done"); px_done = sem("px_done"); rdx_done = sem("rdx_done")
        x2b_done = sem("x2b_done")
        hid_done = sem("hid_done"); gelu_done = sem("gelu_done"); hh_done = sem("hh_done")
        hl_done = [sem("hl_done0"), sem("hl_done1")]
        stored = [sem("stored0"), sem("stored1")]

        block = ctx_.enter_context(nc.Block())

        TURNS = [st for st in ORDER if st[0] in "MWXACEG"]
        RESULTS = [st for st in ORDER if st[0] in "KUVBDFI"]
        SUMS = [st for st in ORDER if st[0] in "BFI"]
        ENDS = [st for st in ORDER if st[0] in ("L1", "L2", "L3")]

        SUM_OF = {"L1": "B", "L2": "F", "L3": "I"}
        END_OF = {s: l for l, s in SUM_OF.items()}

        def count(uses, stage, b):
            return uses.index((stage, b)) + 1

        def tp_of(stage, b):
            return banks[:, bank_tp[(count(TURNS, stage, b) - 1) % 2], :]

        def bank_of(stage, b):
            return (count(RESULTS, stage, b) - 1) % 2

        def piece(n):
            width = 2 * CC * FF // PIECES
            n %= PIECES // 2
            return slice(n * width, (n + 1) * width)

        def tp_read(eng, stage, b):
            use = count(TURNS, stage, b)
            eng.wait_ge(tp_free[(use - 1) % 2], (use + 1) // 2)

        def tp_freed(stage, b):
            return tp_free[(count(TURNS, stage, b) - 1) % 2]

        def quads(stage):
            return range(QUADS // 2) if stage[1] == "a" else range(QUADS // 2, QUADS)

        def cols(b):
            return slice(b * N, (b + 1) * N)

        def hidden(part, f, g):
            return part[:, f, HOME[g]:HOME[g] + FFN[g] * N]

        def piece_side_chunk(n):
            return n // (2 * CC), n // CC % 2, n % CC

        def piece_cols(p):
            return slice(START[p] * N, START[p + 1] * N)

        def in_stack(stack, head, b):
            p = sum(b >= start for start in START[1:])
            return stack[p][:, head, (b - START[p]) * N:(b - START[p] + 1) * N]

        def parts_gone(eng):
            for p in range(len(STACKS)):
                for side in range(2):
                    eng.wait_ge(parted[p][side], 16)

        @block.sync
        def _(sp):
            xv = xT.rearrange("(c p) n -> p c n", p=P)
            sp.dma_start(wq[:, :, :], WqT.rearrange("(c p) n -> p c n", p=P)).then_inc(in_wq, 16)
            sp.dma_start(xT_sb[:, :, piece_cols(0)], xv[:, :, piece_cols(0)]).then_inc(in_xT[0], 16)
            sp.dma_start(wk[:, :, :], WkT.rearrange("(c p) n -> p c n", p=P)).then_inc(in_wk, 16)
            sp.dma_start(xT_sb[:, :, piece_cols(1)], xv[:, :, piece_cols(1)]).then_inc(in_xT[1], 16)
            sp.dma_start(wv[:, :, :], WvT.rearrange("(c p) n -> p c n", p=P)).then_inc(in_wv, 16)
            for p in range(2, len(STACKS)):
                sp.dma_start(xT_sb[:, :, piece_cols(p)], xv[:, :, piece_cols(p)]).then_inc(in_xT[p], 16)

            def write_parts(p, side):
                sp.wait_ge(part3_done, CC * (2 * p + side + 1))
                sp.dma_start(parts[p][side].rearrange("r (c p) n -> p (r c) n", p=P),
                             qk[p][:, side, :, :]).then_inc(parted[p][side], 16)

            def read_stack(p):
                for side, (dst, runs) in enumerate(((qs[p], Q_RUNS), (ks[p], K_RUNS))):
                    sp.wait_ge(parted[p][side], 16)
                    rows = parts[p][side].rearrange("r (d h) n -> (r d) h n", d=D)
                    for group, part, length in runs:
                        sp.dma_start(dst[group * D:(group + length) * D, :, :],
                                     rows[part * D:(part + length) * D, :, :]).then_inc(stacked[p], 16)

            def load_context(b):
                if b >= CR:
                    sp.wait_ge(mm_done, count(RESULTS, "F", b - CR))
                sp.dma_start(ctxT_sb[:, :, b % CR, :],
                             ctxT[b].rearrange("(c p) s -> p c s", p=P)).then_inc(in_ctxT[b], 16)
                sp.dma_start(ctx_sb[:, :, b % CR, :],
                             ctx[b].rearrange("(c p) n -> p c n", p=SP_)).then_inc(in_ctx[b], 16)

            for stage, b in ORDER:
                if stage == "K":
                    p, i = b // (2 * CC), b % (2 * CC)
                    if i == CC:
                        write_parts(p, 0)
                    if i == 2 * CC - 1:
                        write_parts(p, 1)
                if stage == "R":
                    read_stack(b)
                if stage == "Load" and b == 0:
                    sp.dma_start(wo[:, :, :], WoT.rearrange("(c p) n -> p c n", p=P)).then_inc(in_wo, 16)
                    sp.dma_start(x_sb[:, :, :], x.rearrange("b n c -> n b c")).then_inc(in_x, 16)
                    sp.dma_start(bo_bc[:, :], bo.partition_broadcast(N)).then_inc(in_x, 16)
                    sp.dma_start(b2_bc[:, :], b2.partition_broadcast(N)).then_inc(in_x, 16)
                    sp.dma_start(b1_sb[:, :], b1).then_inc(in_b1, 16)
                if stage == "J":
                    load_context(b)
                if stage == "Load" and b == 1:
                    sp.dma_start(w1[:, :].rearrange("p (c f) -> p c f", c=CC),
                                 W1T.rearrange("(c p) f -> p c f", p=P)).then_inc(in_ffn, 16)
                    sp.dma_start(w2[:, :].rearrange("p (c n) -> p c n", c=FC),
                                 W2T.rearrange("(c p) n -> p c n", p=P)).then_inc(in_ffn, 16)
                if stage == "L3":
                    sp.wait_ge(ln_done, count(ENDS, "L3", b))
                    sp.dma_start(out[b], o_sb[:, b % 2, :]).then_inc(stored[b % 2], 16)
            for k in range(2):
                sp.wait_ge(stored[k], 16 * (NB // 2))

        @block.gpsimd
        def _(pool):
            pool.memset(ones[:, :], 1.0).then_inc(ones_ready, 1)
            pool.memset(half_neg[:, :], -0.5).then_inc(const_ready, 1)
            pool.memset(identf[:, :], 0.0).then_inc(const_step, 1)
            pool.memset(identb[:, :], 0.0).then_inc(const_step, 1)
            pool.wait_ge(const_step, 2)
            for ident in (identf, identb):
                pool.affine_select(out=ident[:, :], in_=ident[:, :], compare_op=ALU.not_equal, fill=1.0,
                                   base=0, pattern=[[-1, P]], channel_multiplier=1).then_inc(const_ready, 1)
            pool.memset(sel[:, :, :], 0.0).then_inc(sel_done, 1)
            for r in range(2):
                pool.wait_ge(sel_done, r + 1)
                pool.affine_select(out=sel[:, :, :], in_=sel[:, :, :], compare_op=ALU.not_equal, fill=-1.0,
                                   base=-r * HEADS, pattern=[[-1, HEADS], [0, N]],
                                   channel_multiplier=1).then_inc(sel_done, 1)
            pool.wait_ge(sel_done, 3)
            pool.memset(v_sb[:, :, :, D:], 0.0).then_inc(const_step, 1)
            pool.wait_ge(const_step, 3)
            pool.memset(v_sb[:, :, :, D:D + 1], 1.0).then_inc(const_ready, 1)

            pool.wait_ge(in_x, 48)
            pool.tensor_tensor(x_sb[:, :, :], x_sb[:, :, :],
                               bo_bc[:, :].unsqueeze(1).broadcast_to((N, NB, C)), ALU.add).then_inc(xb_done, 1)

            sums = 0
            for stage, b in ORDER:
                if stage in ("B", "F", "I"):
                    k = sums % 3
                    sums += 1
                    pool.wait_ge(var_done, sums)
                    pool.tensor_scalar(rstd[:, k, 0:1], mv[:, k, 1:2], EPS, None, ALU.add).then_inc(eps_done, 1)
                    pool.wait_ge(eps_done, sums)
                    pool.tensor_tensor(rstd[:, k, 1:2], rstd[:, k, 0:1], half_neg[0:N, :],
                                       ALU.pow).then_inc(rstd_done, 1)
                if stage == "N":
                    if b == 0:
                        pool.wait_ge(thr_done, 2)
                    n, cs = b // (PIECES // 2), piece(b)
                    if n:
                        pool.wait_ge(tern_done, b - PIECES // 2 + 1)
                    pool.tensor_scalar(wtmp[:, cs], (w1, w2)[n][:, cs], thr[:, 2 + n:3 + n], None,
                                       ALU.is_lt).then_inc(tern_step, 1)
                if stage == "H" and b % 2 == 1:
                    g, f = b // FC, b % FC
                    tokens = FFN[g] * N
                    pool.wait_ge(hh_done, b + 1)
                    pool.tensor_tensor(hidden(hl, f, g), h[:, b % HR, 0:tokens],
                                       hidden(hh, f, g).bitcast(F32), ALU.subtract).then_inc(hl_done[1], 1)
                if stage == "G":
                    pool.wait_ge(turned, count(TURNS, "G", b))
                    pool.tensor_tensor(x2[:, b, :], x2[:, b, :], b2_bc[:, :], ALU.add).then_inc(x2b_done, 1)

        @block.scalar
        def _(act):
            def part2(n):
                p, side, c = piece_side_chunk(n)
                act.wait_ge(rest_done, n + 1)
                act.activation(qk[p][:, side, CC + c, :], rest[:, n % 2, 0:STACKS[p] * N],
                               ACT.Copy).then_inc(part2_done, 1)

            for stage, b in ORDER:
                if stage == "K":
                    p, side, c = piece_side_chunk(b)
                    act.wait_ge(mm_done, count(RESULTS, "K", b))
                    act.activation(qk[p][:, side, c, :], banks[:, bank_mm[bank_of("K", b)], 0:STACKS[p] * N],
                                   ACT.Copy).then_inc(part1_done, 1)
                    if b % (2 * CC):
                        part2(b - 1)
                    if (b + 1) % (2 * CC) == 0:
                        part2(b)
                if stage == "U":
                    if b == 0:
                        act.wait_ge(const_ready, 4)
                    act.wait_ge(mm_done, count(RESULTS, "U", b))
                    act.activation(v_sb[:, b, :, 0:D],
                                   banks[0:N, bank_mm[bank_of("U", b)], 0:C].rearrange("n (h d) -> n h d", d=D),
                                   ACT.Copy).then_inc(v_kept, 1)
                if stage == "Z":
                    act.wait_ge(in_ffn, 32)
                    if b:
                        act.wait_ge(wsum_done, 1)
                    act.activation(wtmp[:, :], (w1, w2)[b][:, :], ACT.Abs,
                                   accum_out=wsum[:, b:b + 1]).then_inc(wsum_done, 1)
                if stage in ("Ta", "Tb"):
                    for q in quads(stage):
                        n = QUADS * b + q
                        act.wait_ge(t_done, n + 1)
                        if b >= 2:
                            act.wait_ge(mm_done, count(RESULTS, "V", b - 2))
                        act.activation(pT[:, b % 2, 4 * q:4 * q + 4, :],
                                       banks[0:N, bank_t[n % 2], 0:4 * N].rearrange("k (h n) -> k h n", n=N),
                                       ACT.Exp, scale=float(D) ** -0.5).then_inc(exp_done, 1)
                if stage == "V":
                    act.wait_ge(mm_done, count(RESULTS, "V", b))
                    if b == 0:
                        parts_gone(act)
                    if b >= 2:
                        act.wait_ge(turned, count(TURNS, "W", b - 2))
                    act.activation(pv[:, b % 2, :], banks[:, bank_mm[bank_of("V", b)], 0:4 * N],
                                   ACT.Copy).then_inc(pv_kept, 1)
                if stage in ("A", "C"):
                    use = count(TURNS, stage, b)
                    act.wait_ge(turned, use)
                    if b >= 2:
                        act.wait_ge(mm_done, count(RESULTS, "B" if stage == "A" else "D", b - 2))
                    act.activation((aT if stage == "A" else x1T)[:, b % 2, :, :],
                                   tp_of(stage, b)[:, 0:CC * N].rearrange("p (c n) -> p c n", n=N),
                                   ACT.Copy).then_inc(tp_freed(stage, b), 1)
                if stage == "D":
                    act.wait_ge(nmax_done, b + 1)
                    if b >= 2:
                        act.wait_ge(turned, count(TURNS, "E", b - 2))
                        act.wait_ge(rdx_done, b - 1)
                    act.activation(px[:, b % 2, :], banks[0:N, bank_mm[bank_of("D", b)], 0:S], ACT.Exp,
                                   bias=nmax[:, b % 2:b % 2 + 1],
                                   accum_out=den[:, b % 2:b % 2 + 1]).then_inc(px_done, 1)
                if stage == "E":
                    act.wait_ge(turned, count(TURNS, "E", b))
                    if b >= 2:
                        act.wait_ge(mm_done, count(RESULTS, "F", b - 2))
                    act.activation(pxT[:, b % 2, :, :],
                                   tp_of(stage, b)[0:SP_, 0:SC * N].rearrange("p (c n) -> p c n", n=N),
                                   ACT.Copy).then_inc(tp_freed(stage, b), 1)
                if stage == "G":
                    act.wait_ge(turned, count(TURNS, "G", b))
                    if b == 0:
                        act.wait_ge(mm_done, count(RESULTS, "U", NB - 1))
                    act.activation(x2h[:, :, cols(b)],
                                   tp_of(stage, b)[:, 0:CC * N].rearrange("p (c n) -> p c n", n=N),
                                   ACT.Copy).then_inc(x2h_done, 1)
                if stage == "H":
                    if b == 0:
                        act.wait_ge(in_b1, 16)
                    act.wait_ge(hid_done, b + 1)
                    if b >= HR:
                        act.wait_ge(hl_done[b % 2], (b - HR) // 2 + 1)
                    tokens = FFN[b // FC] * N
                    bank = bank_s[b % 2] if b < FC else (bank_s + bank_t)[b % 4]
                    act.activation(h[:, b % HR, 0:tokens], banks[:, bank, 0:tokens], ACT.Gelu,
                                   bias=b1_sb[:, b % FC:b % FC + 1]).then_inc(gelu_done, 1)

        @block.vector
        def _(dve):
            def part3(n):
                p, side, c = piece_side_chunk(n)
                dve.wait_ge(part2_done, n + 1)
                dve.tensor_tensor(qk[p][:, side, 2 * CC + c, :], rest[:, n % 2, 0:STACKS[p] * N],
                                  qk[p][:, side, CC + c, :], ALU.subtract).then_inc(part3_done, 1)

            sums = 0

            def statistics(k):
                dve.wait_ge(y_done, sums)
                dve.bn_stats(stats[:, k, :], y[:, k, :]).then_inc(bn_done, 1)
                dve.wait_ge(bn_done, sums)
                dve.bn_aggr(mv[:, k, :], stats[:, k, :]).then_inc(var_done, 1)

            for stage, b in ORDER:
                if stage == "K":
                    p, side, c = piece_side_chunk(b)
                    dve.wait_ge(part1_done, b + 1)
                    if b >= 2:
                        dve.wait_ge(part3_done, b - 1)
                    dve.tensor_tensor(rest[:, b % 2, 0:STACKS[p] * N],
                                      banks[:, bank_mm[bank_of("K", b)], 0:STACKS[p] * N],
                                      qk[p][:, side, c, :], ALU.subtract).then_inc(rest_done, 1)
                    if b % (2 * CC):
                        part3(b - 1)
                    if (b + 1) % (2 * CC) == 0:
                        part3(b)
                if stage == "X":
                    dve.wait_ge(turned, count(TURNS, "X", 0))
                    dve.tensor_scalar(thr[:, 4:6], tp_of(stage, b)[:, 0:2], 1.0 / (C * FF), 1e-8,
                                      ALU.mult, ALU.max).then_inc(tp_freed(stage, b), 1)
                    tp_read(dve, "X", 0)
                    dve.tensor_scalar(thr[:, 0:2], thr[:, 4:6], 0.5, None, ALU.mult).then_inc(thr_done, 1)
                    dve.tensor_scalar(thr[:, 2:4], thr[:, 4:6], -0.5, None, ALU.mult).then_inc(thr_done, 1)
                if stage == "Y":
                    if b == 0:
                        dve.wait_ge(thr_done, 2)
                    n, cs = b // (PIECES // 2), piece(b)
                    w, t = (w1, t1) if n == 0 else (w2, t2)
                    dve.wait_ge(tern_step, b + 1)
                    dve.scalar_tensor_tensor(t[:, :, :].rearrange("p c n -> p (c n)")[:, cs], w[:, cs],
                                             thr[:, n:n + 1], wtmp[:, cs], ALU.is_gt,
                                             ALU.subtract).then_inc(tern_done, 1)
                if stage in ("Sa", "Sb"):
                    if b >= 2:
                        dve.wait_ge(mcat_done, b - 1)
                    for q in quads(stage):
                        n = QUADS * b + q
                        dve.wait_ge(s_done, n + 1)
                        dve.tensor_reduce(mx[:, b % 2, 4 * q:4 * q + 4],
                                          banks[0:N, bank_s[n % 2], 0:4 * N].rearrange("q (h k) -> q h k", k=N),
                                          AX.X, ALU.max).then_inc(max_done, 1)
                if stage == "Sb":
                    dve.wait_ge(max_done, QUADS * (b + 1))
                    dve.tensor_copy(mcat[:, b % 2, 0:HEADS], mx[:, b % 2, :]).then_inc(mcat_step, 1)
                    dve.wait_ge(mcat_step, b + 1)
                    dve.tensor_tensor(mcat[:, b % 2, HEADS:2 * HEADS], mx[:, b % 2, :],
                                      mcat[:, b % 2, 0:HEADS], ALU.subtract).then_inc(mcat_done, 1)
                if stage == "M":
                    dve.wait_ge(turned, count(TURNS, "M", b))
                    if b >= 2:
                        dve.wait_ge(t_done, QUADS * (b - 1))
                    dve.tensor_copy(mT[:, b % 2, :],
                                    tp_of(stage, b)[0:2 * HEADS, 0:N // 2].bitcast(BF16)).then_inc(tp_freed(stage, b), 1)
                if stage == "W":
                    av = tp_of(stage, b)[0:N, :].rearrange("n (h e) -> n h e", e=32)
                    dve.wait_ge(turned, count(TURNS, "W", b))
                    if b >= 2:
                        tp_read(dve, "W", b - 2)
                    dve.reciprocal(rden[:, b % 2, :], av[:, :, D]).then_inc(rden_done, 1)
                    if b >= 2:
                        dve.wait_ge(turned, count(TURNS, "A", b - 2))
                    dve.wait_ge(rden_done, b + 1)
                    dve.tensor_tensor(a_sb[:, b % 2, :].rearrange("n (h d) -> n h d", d=D), av[:, :, 0:D],
                                      rden[:, b % 2, :].unsqueeze(2).broadcast_to((N, HEADS, D)),
                                      ALU.mult).then_inc(tp_freed(stage, b), 1)
                if stage == "D":
                    dve.wait_ge(mm_done, count(RESULTS, "D", b))
                    if b >= 2:
                        dve.wait_ge(px_done, b - 1)
                    dve.tensor_reduce(nmax[:, b % 2:b % 2 + 1], banks[0:N, bank_mm[bank_of("D", b)], 0:S],
                                      AX.X, ALU.max, negate=True).then_inc(nmax_done, 1)
                if stage == "E":
                    dve.wait_ge(px_done, b + 1)
                    dve.reciprocal(rdx[:, b % 2:b % 2 + 1], den[:, b % 2:b % 2 + 1]).then_inc(rdx_done, 1)
                if stage in ("B", "F", "I"):
                    k = sums % 3
                    sums += 1
                    bank = bank_of(stage, b)
                    if sums == 1:
                        parts_gone(dve)
                    dve.wait_ge(mm_done, count(RESULTS, stage, b))
                    psum = banks[0:N, bank_mm[bank], 0:C]
                    if sums > 3:
                        dve.wait_ge(ln_done, count(ENDS, END_OF[SUMS[sums - 4][0]], SUMS[sums - 4][1]))
                    if stage == "B":
                        if b == 0:
                            dve.wait_ge(xb_done, 1)
                        dve.tensor_tensor(y[:, k, :], psum, x_sb[:, b, :], ALU.add).then_inc(y_done, 1)
                    if stage == "F":
                        dve.wait_ge(rdx_done, b + 1)
                        dve.scalar_tensor_tensor(y[:, k, :], psum, rdx[:, b % 2:b % 2 + 1], x1[:, b % 3, :],
                                                 ALU.mult, ALU.add).then_inc(y_done, 1)
                    if stage == "I":
                        dve.wait_ge(x2b_done, b + 1)
                        dve.tensor_tensor(y[:, k, :], psum, x2[:, b, :], ALU.add).then_inc(y_done, 1)
                    statistics(k)
                if stage in ("L1", "L2", "L3"):
                    use = count(SUMS, SUM_OF[stage], b)
                    k = (use - 1) % 3
                    dve.wait_ge(rstd_done, use)
                    if stage == "L1":
                        if b >= 3:
                            dve.wait_ge(turned, count(TURNS, "C", b - 3))
                        to = x1[:, b % 3, :]
                    if stage == "L2":
                        to = x2[:, b, :]
                    if stage == "L3":
                        if b >= 2:
                            dve.wait_ge(stored[b % 2], 16 * (b // 2))
                        to = o_sb[:, b % 2, :]
                    dve.tensor_scalar(to, y[:, k, :], mv[:, k, 0:1], rstd[:, k, 1:2], ALU.subtract,
                                      ALU.mult).then_inc(ln_done, 1)
                if stage == "G":
                    dve.wait_ge(x2h_done, b + 1)
                    if b == 0:
                        dve.wait_ge(mm_done, count(RESULTS, "U", NB - 1))
                    dve.tensor_tensor(x2l[:, :, cols(b)],
                                      tp_of(stage, b)[:, 0:CC * N].rearrange("p (c n) -> p c n", n=N),
                                      x2h[:, :, cols(b)], ALU.subtract).then_inc(tp_freed(stage, b), 1)
                if stage == "H":
                    g, f = b // FC, b % FC
                    tokens = FFN[g] * N
                    if b == 0:
                        dve.wait_ge(tern_done, PIECES)
                    elif f == 0:
                        dve.wait_ge(mm_done, count(RESULTS, "I", FIRST[g if HOME[g] == 0 else g - 1] - 1))
                    dve.wait_ge(gelu_done, b + 1)
                    dve.tensor_copy(hidden(hh, f, g), h[:, b % HR, 0:tokens]).then_inc(hh_done, 1)
                    if f % 2 == 0:
                        dve.wait_ge(hh_done, b + 1)
                        dve.tensor_tensor(hidden(hl, f, g), h[:, b % HR, 0:tokens],
                                          hidden(hh, f, g).bitcast(F32), ALU.subtract).then_inc(hl_done[0], 1)

        @block.tensor
        def _(pe):
            def bank_tp_ready(stage, b):
                use = count(TURNS, stage, b)
                if use > 2:
                    pe.wait_ge(tp_free[(use - 1) % 2], (use - 1) // 2)

            def bank_mm_ready(stage, b):
                use = count(RESULTS, stage, b)
                if use > 2:
                    last, lb = RESULTS[use - 3]
                    if last == "D":
                        pe.wait_ge(px_done, lb + 1)
                    elif last == "K":
                        pe.wait_ge(rest_done, lb + 1)
                    elif last == "U":
                        pe.wait_ge(v_kept, lb + 1)
                    elif last == "V":
                        pe.wait_ge(pv_kept, lb + 1)
                    else:
                        pe.wait_ge(y_done, count(SUMS, last, lb))
                return banks[0:N, bank_mm[(use - 1) % 2], :]

            def turn(to, src, rows, parts):
                for c in range(parts):
                    w = src.shape[1] // parts
                    mm = pe.transpose(to[0:w, c * rows:(c + 1) * rows],
                                      src[:, c * w:(c + 1) * w], identf[0:rows, 0:rows])
                mm.then_inc(turned, 1)

            pe.wait_ge(ones_ready, 1)
            for _ in range(WARM_UP):
                pe.matmul(banks[:, bank_t[1], 0:P], ones[:, :], ones[:, :], start=True, stop=True)

            for stage, b in ORDER:
                if stage == "K":
                    p, side, m = piece_side_chunk(b)
                    if side == 0 and m == 0:
                        pe.wait_ge(in_xT[p], 16)
                    if p == 0 and m == 0:
                        pe.wait_ge((in_wq, in_wk)[side], 16)
                    bank_mm_ready("K", b)
                    for c in range(CC):
                        mm = pe.matmul(banks[:, bank_mm[bank_of("K", b)], 0:STACKS[p] * N],
                                       (wq, wk)[side][:, c, m * P:(m + 1) * P],
                                       xT_sb[:, c, piece_cols(p)], start=(c == 0), stop=(c == CC - 1))
                    mm.then_inc(mm_done, 1)
                if stage == "U":
                    if b == 0:
                        pe.wait_ge(in_wv, 16)
                    to = bank_mm_ready("U", b)
                    for c in range(CC):
                        mm = pe.matmul(to[:, 0:C], xT_sb[:, c, cols(b)], wv[:, c, :],
                                       start=(c == 0), stop=(c == CC - 1))
                    mm.then_inc(mm_done, 1)
                if stage == "X":
                    pe.wait_ge(wsum_done, 2)
                    bank_tp_ready("X", 0)
                    pe.matmul(tp_of(stage, b)[:, 0:2], ones[:, :], wsum[:, 0:2],
                              start=True, stop=True).then_inc(turned, 1)
                if stage in ("Sa", "Sb"):
                    if stage == "Sa" and b == 0:
                        pe.wait_ge(const_ready, 4)
                    if stage == "Sa" and b in START:
                        pe.wait_ge(stacked[START.index(b)], 16 * (len(Q_RUNS) + len(K_RUNS)))
                    for q in quads(stage):
                        n = QUADS * b + q
                        if n >= 2:
                            pe.wait_ge(max_done, n - 1)
                        for j in range(4):
                            mm = pe.matmul(banks[0:N, bank_s[n % 2], j * N:(j + 1) * N],
                                           in_stack(qs, 4 * q + j, b), in_stack(ks, 4 * q + j, b),
                                           start=True, stop=True)
                        mm.then_inc(s_done, 1)
                if stage == "M":
                    pe.wait_ge(mcat_done, b + 1)
                    bank_tp_ready("M", b)
                    pe.transpose(tp_of(stage, b)[0:2 * HEADS, 0:N // 2].bitcast(BF16), mcat[:, b % 2, :],
                                 identb[0:N, 0:N]).then_inc(turned, 1)
                if stage in ("Ta", "Tb"):
                    if b == 0:
                        pe.wait_ge(sel_done, 3)
                    tp_read(pe, "M", b)
                    for q in quads(stage):
                        n = QUADS * b + q
                        if n >= 2:
                            pe.wait_ge(exp_done, n - 1)
                        for j in range(4):
                            to = banks[0:N, bank_t[n % 2], j * N:(j + 1) * N]
                            pe.matmul(to, in_stack(ks, 4 * q + j, b), in_stack(qs, 4 * q + j, b),
                                      start=True, stop=False)
                            mm = pe.matmul(to, sel[:, 4 * q + j, :], mT[:, b % 2, :],
                                           start=False, stop=True)
                        mm.then_inc(t_done, 1)
                if stage == "V":
                    pe.wait_ge(exp_done, QUADS * (b + 1))
                    pe.wait_ge(v_kept, b + 1)
                    bank_mm_ready("V", b)
                    for hd in range(HEADS):
                        r, j = hd // 4, hd % 4
                        mm = pe.matmul(banks[32 * j:32 * j + 32, bank_mm[bank_of("V", b)], r * N:(r + 1) * N],
                                       v_sb[:, b, hd, :], pT[:, b % 2, hd, :], start=True, stop=True)
                    mm.then_inc(mm_done, 1)
                if stage == "W":
                    pe.wait_ge(pv_kept, b + 1)
                    bank_tp_ready("W", b)
                    for r in range(HEADS // 4):
                        mm = pe.transpose(tp_of(stage, b)[0:N, r * P:(r + 1) * P],
                                          pv[:, b % 2, r * N:(r + 1) * N], identf[:, :])
                    mm.then_inc(turned, 1)
                if stage == "A":
                    tp_read(pe, "W", b)
                    bank_tp_ready("A", b)
                    turn(tp_of(stage, b), a_sb[:, b % 2, :], N, CC)
                if stage == "B":
                    tp_read(pe, "A", b)
                    if b == 0:
                        pe.wait_ge(in_wo, 16)
                    to = bank_mm_ready("B", b)
                    for c in range(CC):
                        mm = pe.matmul(to[:, 0:C], aT[:, b % 2, c, :], wo[:, c, :],
                                       start=(c == 0), stop=(c == CC - 1))
                    mm.then_inc(mm_done, 1)
                if stage == "C":
                    pe.wait_ge(ln_done, count(ENDS, "L1", b))
                    bank_tp_ready("C", b)
                    turn(tp_of(stage, b), x1[:, b % 3, :], N, CC)
                if stage == "D":
                    tp_read(pe, "C", b)
                    pe.wait_ge(in_ctxT[b], 16)
                    to = bank_mm_ready("D", b)
                    for c in range(CC):
                        mm = pe.matmul(to[:, 0:S], x1T[:, b % 2, c, :], ctxT_sb[:, c, b % CR, :],
                                       start=(c == 0), stop=(c == CC - 1))
                    mm.then_inc(mm_done, 1)
                if stage == "E":
                    pe.wait_ge(px_done, b + 1)
                    bank_tp_ready("E", b)
                    turn(tp_of(stage, b), px[:, b % 2, :], N, SC)
                if stage == "F":
                    tp_read(pe, "E", b)
                    pe.wait_ge(in_ctx[b], 16)
                    to = bank_mm_ready("F", b)
                    for c in range(SC):
                        mm = pe.matmul(to[:, 0:C], pxT[:, b % 2, c, :], ctx_sb[:, c, b % CR, :],
                                       start=(c == 0), stop=(c == SC - 1))
                    mm.then_inc(mm_done, 1)
                if stage == "G":
                    pe.wait_ge(ln_done, count(ENDS, "L2", b))
                    bank_tp_ready("G", b)
                    turn(tp_of(stage, b), x2[:, b, :], N, CC)
                if stage == "H":
                    g, f = b // FC, b % FC
                    if b == 0:
                        pe.wait_ge(max_done, QUADS * NB)
                        pe.wait_ge(tern_done, PIECES // 2)
                    tp_read(pe, "G", FIRST[g + 1] - 1)
                    bank = banks[:, bank_s[b % 2] if g == 0 else (bank_s + bank_t)[b % 4], :]
                    if b == FC:
                        pe.wait_ge(exp_done, QUADS * NB)
                    if b >= 2:
                        pe.wait_ge(gelu_done, b - 1 if b < FC + 2 else b - 3)
                    mms = [(c, part) for c in range(CC) for part in (x2h, x2l)]
                    for i, (c, part) in enumerate(mms):
                        mm = pe.matmul(bank[:, 0:FFN[g] * N], t1[:, c, f * P:(f + 1) * P],
                                       part[:, c, FIRST[g] * N:FIRST[g + 1] * N],
                                       start=(i == 0), stop=(i == len(mms) - 1))
                    mm.then_inc(hid_done, 1)
                if stage == "I":
                    to = bank_mm_ready("I", b)
                    if b == 0:
                        pe.wait_ge(tern_done, PIECES)
                    mms = [(f, part) for f in range(FC) for part in (hh, hl)]
                    for i, (f, part) in enumerate(mms):
                        g = GROUP_OF[b]
                        if b == FIRST[g]:
                            pe.wait_ge(hl_done[f % 2], (FC * g + f) // 2 + 1)
                        first = HOME[g] + (b - FIRST[g]) * N
                        mm = pe.matmul(to[:, 0:C], part[:, f, first:first + N], t2[:, f, :],
                                       start=(i == 0), stop=(i == len(mms) - 1))
                    mm.then_inc(mm_done, 1)

    return nc


def kernel(**inputs):
    import numpy as np
    import concourse.bacc as bacc
    from concourse.bass_utils import run_bass_kernel_spmd

    a = {k: np.asarray(v) for k, v in inputs.items()}

    def turned(m):
        return np.ascontiguousarray(np.moveaxis(m, -1, -2))

    def by_depth(m):
        return np.moveaxis(m.reshape(HEADS, -1, m.shape[-1]), 0, 1).reshape(m.shape)

    x, ctx = a["x"], a["ctx_1024"]
    arrays = {
        "x": x,
        "xT": turned(x.reshape(-1, x.shape[-1])),
        "ctx": ctx,
        "ctxT": turned(ctx),
        "WqT": turned(by_depth(a["L0_attn_Wq"])), "WkT": turned(by_depth(a["L0_attn_Wk"])),
        "WvT": turned(a["L0_attn_Wv"]),
        "WoT": turned(a["L0_attn_Wout"]), "bo": a["L0_attn_bout"],
        "W1T": turned(a["L0_ffn_W1"]), "b1": turned(a["L0_ffn_b1"].reshape(-1, P)),
        "W2T": turned(a["L0_ffn_W2"]), "b2": a["L0_ffn_b2"],
    }
    arrays = {f"in_{k}": np.ascontiguousarray(v) for k, v in arrays.items()}
    nc = bacc.Bacc("TRN2", target_bir_lowering=False, num_devices=1)
    args = [nc.dram_tensor(k, v.shape, mybir.dt.from_np(v.dtype), kind="ExternalInput").ap()
            for k, v in arrays.items()]
    args.append(nc.dram_tensor("out", x.shape, F32, kind="ExternalOutput").ap())
    decoder_layer(nc, *args)
    r = run_bass_kernel_spmd(nc, [arrays], core_ids=[0])
    return r.results[0]["out"]
```
